# Optimizing a Trainium2 kernel written in Bass

```python
import numpy as np
import jax
import jax.numpy as jnp

def _softmax(x, axis=-1):
    return jax.nn.softmax(x, axis=axis)

def _gelu(x):
    return jax.nn.gelu(x, approximate=True)

def _silu(x):
    return jax.nn.silu(x)

def _sigmoid(x):
    return jax.nn.sigmoid(x)

def _layernorm(x, axis=-1, eps=1e-05):
    m = jnp.mean(x, axis=axis, keepdims=True)
    v = jnp.var(x, axis=axis, keepdims=True)
    return (x - m) / jnp.sqrt(v + eps)

def _scatter_add(tgt, idx, src, axis=0):
    return tgt.at[idx].add(src)

def _segment_sum(src, seg, n):
    return jax.ops.segment_sum(src, seg, n)
kernel_name = 'mk_vit_tower_d1_tok_img256_r4_06f017'

def setup_inputs(seed: int=0):
    np.random.seed(seed)
    _w = jnp.asarray

    def _rec_inputs():
        import jax
        import jax.numpy as jnp
        _rk = jax.random.key(seed)
        x = -0.00016672 + 0.999947 * jax.random.normal(jax.random.fold_in(_rk, 1), (32, 3, 64, 64), jnp.float32)
        return x
    x = _rec_inputs()

    def _L0_tok_setup():
        import jax, jax.numpy as jnp
        import numpy as np
        PATCH = 16
        key = jax.random.key(seed)
        k1, k2, k3 = jax.random.split(key, 3)
        B, C, H, Wd = (64, 3, 96, 96)
        E = 64
        pdim = PATCH * PATCH * C
        x = jax.random.normal(k1, (B, C, H, Wd), dtype=jnp.float32)
        W = jax.random.normal(k2, (E, pdim), dtype=jnp.float32) * pdim ** (-0.5)
        b = jax.random.normal(k3, (E,), dtype=jnp.float32) * 0.01
        return {'x': x, 'W': W, 'b': b}
    _L0_tok_all = _L0_tok_setup()
    _L0_tok_in = {k: v for k, v in _L0_tok_all.items() if k in ('W', 'b')}
    del _L0_tok_all

    def _L0_attn_setup():
        import jax, jax.numpy as jnp
        import numpy as np
        DIM = 64
        HEADS = 8
        DIM_HEAD = 32
        LANDMARKS = 128
        PINV_ITERS = 6
        KERNEL = 33
        SCALE = DIM_HEAD ** (-0.5)
        LN_EPS = 1e-05

        def _pinv(a, iters=PINV_ITERS):
            abs_a = jnp.abs(a)
            col = jnp.max(abs_a.sum(axis=-1))
            row = jnp.max(abs_a.sum(axis=-2))
            z = jnp.swapaxes(a, -1, -2) / (col * row)
            I = jnp.eye(a.shape[-1], dtype=a.dtype)
            for _ in range(iters):
                az = a @ z
                z = 0.25 * z @ (13.0 * I - az @ (15.0 * I - az @ (7.0 * I - az)))
            return z

        def _reference_tuple_inner(x, ln_g, ln_b, w_qkv, w_out, b_out, res_kernel):
            b, n, d = x.shape
            mu = jnp.mean(x, -1, keepdims=True)
            var = jnp.var(x, -1, keepdims=True)
            xn = (x - mu) * jax.lax.rsqrt(var + LN_EPS) * ln_g + ln_b
            pad = -n % LANDMARKS
            xp = jnp.pad(xn, ((0, 0), (pad, 0), (0, 0)))
            N = n + pad
            qkv = xp @ w_qkv
            q, k, v = jnp.split(qkv, 3, axis=-1)
            to_h = lambda t: t.reshape(b, N, HEADS, DIM_HEAD).transpose(0, 2, 1, 3)
            q = to_h(q) * SCALE
            k = to_h(k)
            v = to_h(v)
            l = N // LANDMARKS
            q_l = q.reshape(b, HEADS, LANDMARKS, l, DIM_HEAD).mean(3)
            k_l = k.reshape(b, HEADS, LANDMARKS, l, DIM_HEAD).mean(3)
            attn1 = jax.nn.softmax(jnp.einsum('bhid,bhjd->bhij', q, k_l), -1)
            attn2 = jax.nn.softmax(jnp.einsum('bhid,bhjd->bhij', q_l, k_l), -1)
            attn3 = jax.nn.softmax(jnp.einsum('bhid,bhjd->bhij', q_l, k), -1)
            attn2_inv = _pinv(attn2)
            a12 = attn1 @ attn2_inv
            out = a12 @ (attn3 @ v)
            res = jax.lax.conv_general_dilated(v, res_kernel, (1, 1), ((KERNEL // 2, KERNEL // 2), (0, 0)), feature_group_count=HEADS, dimension_numbers=('NCHW', 'OIHW', 'NCHW'))
            out = out + res
            out = out.transpose(0, 2, 1, 3).reshape(b, N, HEADS * DIM_HEAD)
            out = out @ w_out + b_out
            out = out[:, -n:]
            att = a12 @ attn3
            return (x + out, att, pad, n)
        key = jax.random.key(seed)
        ks = jax.random.split(key, 4)
        b, n = (1, 1000)
        inner = HEADS * DIM_HEAD
        s = 0.02
        return {'x': jax.random.normal(ks[0], (b, n, DIM), jnp.float32), 'ln_g': jnp.ones((DIM,), jnp.float32), 'ln_b': jnp.zeros((DIM,), jnp.float32), 'w_qkv': jax.random.normal(ks[1], (DIM, 3 * inner), jnp.float32) * s, 'w_out': jax.random.normal(ks[2], (inner, DIM), jnp.float32) * s, 'b_out': jnp.zeros((DIM,), jnp.float32), 'res_kernel': jax.random.normal(ks[3], (HEADS, 1, KERNEL, 1), jnp.float32) * s}
    _L0_attn_all = _L0_attn_setup()
    _L0_attn_in = {k: v for k, v in _L0_attn_all.items() if k in ('ln_g', 'ln_b', 'w_qkv', 'w_out', 'b_out', 'res_kernel')}
    del _L0_attn_all

    def _L0_ffn_setup():
        import jax, jax.numpy as jnp
        import numpy as np
        B, S, D, E, H, K = (4, 1024, 64, 8, 128, 2)
        key = jax.random.key(seed)
        ks = jax.random.split(key, 6)
        x = jax.random.normal(ks[0], (B, S, D), jnp.float32)
        Wg = jax.random.normal(ks[1], (D, E), jnp.float32) * 0.02
        bg = jnp.zeros((E,), jnp.float32)
        W1 = jax.random.normal(ks[2], (E, D, H), jnp.float32) * 0.02
        b1 = jnp.zeros((E, H), jnp.float32)
        W2 = jax.random.normal(ks[3], (E, H, D), jnp.float32) * 0.02
        b2 = jnp.zeros((E, D), jnp.float32)
        return {'x': x, 'Wg': Wg, 'bg': bg, 'W1': W1, 'b1': b1, 'W2': W2, 'b2': b2}
    _L0_ffn_all = _L0_ffn_setup()
    _L0_ffn_in = {k: v for k, v in _L0_ffn_all.items() if k in ('Wg', 'bg', 'W1', 'b1', 'W2', 'b2')}
    del _L0_ffn_all
    return {'x': x, 'L0_tok_W': _L0_tok_in['W'], 'L0_tok_b': _L0_tok_in['b'], 'L0_attn_ln_g': _L0_attn_in['ln_g'], 'L0_attn_ln_b': _L0_attn_in['ln_b'], 'L0_attn_w_qkv': _L0_attn_in['w_qkv'], 'L0_attn_w_out': _L0_attn_in['w_out'], 'L0_attn_b_out': _L0_attn_in['b_out'], 'L0_attn_res_kernel': _L0_attn_in['res_kernel'], 'L0_ffn_Wg': _L0_ffn_in['Wg'], 'L0_ffn_bg': _L0_ffn_in['bg'], 'L0_ffn_W1': _L0_ffn_in['W1'], 'L0_ffn_b1': _L0_ffn_in['b1'], 'L0_ffn_W2': _L0_ffn_in['W2'], 'L0_ffn_b2': _L0_ffn_in['b2']}

def reference(x, L0_tok_W, L0_tok_b, L0_attn_ln_g, L0_attn_ln_b, L0_attn_w_qkv, L0_attn_w_out, L0_attn_b_out, L0_attn_res_kernel, L0_ffn_Wg, L0_ffn_bg, L0_ffn_W1, L0_ffn_b1, L0_ffn_W2, L0_ffn_b2):
    import jax
    import jax.numpy as jnp

    def _L0_tok_ref(x, W, b):
        import jax, jax.numpy as jnp
        import numpy as np
        PATCH = 16
        B, C, H, Wd = x.shape
        p = PATCH
        nH, nW = (H // p, Wd // p)
        patches = x.reshape(B, C, nH, p, nW, p)
        patches = patches.transpose(0, 2, 4, 1, 3, 5)
        patches = patches.reshape(B, nH * nW, C * p * p)
        return jnp.einsum('bnk,ek->bne', patches, W) + b

    def _L0_attn_ref(x, ln_g, ln_b, w_qkv, w_out, b_out, res_kernel):
        import jax, jax.numpy as jnp
        import numpy as np
        DIM = 64
        HEADS = 8
        DIM_HEAD = 32
        LANDMARKS = 128
        PINV_ITERS = 6
        KERNEL = 33
        SCALE = DIM_HEAD ** (-0.5)
        LN_EPS = 1e-05

        def _pinv(a, iters=PINV_ITERS):
            abs_a = jnp.abs(a)
            col = jnp.max(abs_a.sum(axis=-1))
            row = jnp.max(abs_a.sum(axis=-2))
            z = jnp.swapaxes(a, -1, -2) / (col * row)
            I = jnp.eye(a.shape[-1], dtype=a.dtype)
            for _ in range(iters):
                az = a @ z
                z = 0.25 * z @ (13.0 * I - az @ (15.0 * I - az @ (7.0 * I - az)))
            return z

        def _reference_tuple_inner(x, ln_g, ln_b, w_qkv, w_out, b_out, res_kernel):
            b, n, d = x.shape
            mu = jnp.mean(x, -1, keepdims=True)
            var = jnp.var(x, -1, keepdims=True)
            xn = (x - mu) * jax.lax.rsqrt(var + LN_EPS) * ln_g + ln_b
            pad = -n % LANDMARKS
            xp = jnp.pad(xn, ((0, 0), (pad, 0), (0, 0)))
            N = n + pad
            qkv = xp @ w_qkv
            q, k, v = jnp.split(qkv, 3, axis=-1)
            to_h = lambda t: t.reshape(b, N, HEADS, DIM_HEAD).transpose(0, 2, 1, 3)
            q = to_h(q) * SCALE
            k = to_h(k)
            v = to_h(v)
            l = N // LANDMARKS
            q_l = q.reshape(b, HEADS, LANDMARKS, l, DIM_HEAD).mean(3)
            k_l = k.reshape(b, HEADS, LANDMARKS, l, DIM_HEAD).mean(3)
            attn1 = jax.nn.softmax(jnp.einsum('bhid,bhjd->bhij', q, k_l), -1)
            attn2 = jax.nn.softmax(jnp.einsum('bhid,bhjd->bhij', q_l, k_l), -1)
            attn3 = jax.nn.softmax(jnp.einsum('bhid,bhjd->bhij', q_l, k), -1)
            attn2_inv = _pinv(attn2)
            a12 = attn1 @ attn2_inv
            out = a12 @ (attn3 @ v)
            res = jax.lax.conv_general_dilated(v, res_kernel, (1, 1), ((KERNEL // 2, KERNEL // 2), (0, 0)), feature_group_count=HEADS, dimension_numbers=('NCHW', 'OIHW', 'NCHW'))
            out = out + res
            out = out.transpose(0, 2, 1, 3).reshape(b, N, HEADS * DIM_HEAD)
            out = out @ w_out + b_out
            out = out[:, -n:]
            att = a12 @ attn3
            return (x + out, att, pad, n)
        return _reference_tuple_inner(x, ln_g, ln_b, w_qkv, w_out, b_out, res_kernel)[0]

    def _L0_ffn_ref(x, Wg, bg, W1, b1, W2, b2):
        import jax, jax.numpy as jnp
        import numpy as np
        B, S, D, E, H, K = (4, 1024, 64, 8, 128, 2)
        Bv, Sv, Dv = x.shape
        gate_scores = x @ Wg + bg
        _, idx = jax.lax.top_k(gate_scores, K)
        mask = jax.nn.one_hot(idx, E, dtype=x.dtype).sum(axis=-2)
        xf = x.reshape(-1, Dv)
        mf = mask.reshape(-1, E)
        h = jax.nn.gelu(jnp.einsum('td,edh->teh', xf, W1) + b1[None], approximate=False)
        y = jnp.einsum('teh,ehd->ted', h, W2) + b2[None]
        out = jnp.einsum('ted,te->td', y, mf)
        return out.reshape(Bv, Sv, Dv)
    h = _L0_tok_ref(x, L0_tok_W, L0_tok_b)
    h = h + _L0_attn_ref(_layernorm(h, axis=-1), L0_attn_ln_g, L0_attn_ln_b, L0_attn_w_qkv, L0_attn_w_out, L0_attn_b_out, L0_attn_res_kernel)
    h = h + _L0_ffn_ref(_layernorm(h, axis=-1), L0_ffn_Wg, L0_ffn_bg, L0_ffn_W1, L0_ffn_b1, L0_ffn_W2, L0_ffn_b2)
    return h

_drawn_inputs = setup_inputs


def setup_inputs(seed=0):
    import zlib

    import numpy as np

    out = dict(_drawn_inputs(seed))
    spreads = {'L0_attn_ln_g': (1.0, 0.6),
     'L0_attn_ln_b': (0.0, 0.8),
     'L0_attn_b_out': (0.0, 0.396),
     'L0_ffn_bg': (0.0, 0.1),
     'L0_ffn_b1': (0.0, 0.8),
     'L0_ffn_b2': (0.0, 0.374)}
    factors = {'L0_tok_b': 4.562,
     'L0_attn_w_qkv': 8.0,
     'L0_attn_w_out': 8.0,
     'L0_attn_res_kernel': 8.0,
     'L0_ffn_W1': 4.358,
     'L0_ffn_W2': 3.669}
    for name, (base, spread) in spreads.items():
        noise = np.random.default_rng([zlib.crc32(name.encode()), seed]).standard_normal(out[name].shape)
        drawn = base * np.exp(spread * noise) if base else spread * noise
        out[name] = jnp.asarray(drawn.astype(out[name].dtype))
    for name, factor in factors.items():
        out[name] = (out[name] * factor).astype(out[name].dtype)
    return out
```

```python
from contextlib import ExitStack

import numpy as np

import concourse.bass as bass
from concourse import mybir

F32 = mybir.dt.float32
BF16 = mybir.dt.bfloat16
F16 = mybir.dt.float16
ALU = mybir.AluOpType
ACT = mybir.ActivationFunctionType
AX = mybir.AxisListType.X

IMAGES = 32
TOKENS = 16
PADS = 112
ROWS = TOKENS + 1
PER_TILE = 7
TILES = -(-IMAGES // PER_TILE)
D = 64
HEADS = 8
DH = 32
CHUNKS = 6
EXPERTS = 8
HIDDEN = 128
ITERS = 6
EPS = 1e-5
BLOCKS = [min(PER_TILE, IMAGES - PER_TILE * t) for t in range(TILES)]
R = [ROWS * n for n in BLOCKS]
OFF = [ROWS * PER_TILE * t for t in range(TILES)]
RMAX = R[0]
ALL_ROWS = ROWS * IMAGES
C = HEADS * ROWS
WIDE = 128
ALPHA = 3.5
FAR = float(2.0 ** 100)

P128 = dict(tokw=CHUNKS * D, wvT=2 * D, woutbd=2 * 4 * D, w2=EXPERTS * D)
P65 = dict(wqk=2 * HEADS * DH, ln=2, wg=EXPERTS, w1=EXPERTS * HIDDEN)
P119 = dict(tokb=D, bout=D, toep=C)
CST = dict(ident=128, blocks=RMAX, wcol=ROWS, wsym=ROWS, eye=ROWS, selw=PER_TILE, winv=ROWS,
           before=EXPERTS * EXPERTS, farl=RMAX, farr=2 * RMAX)


def starts(widths):
    out, at = {}, 0
    for name, w in widths.items():
        out[name] = (at, at + w)
        at += w
    return out, at


def vit_layer(nc, x_in, p128_in, p65_in, p119_in, b2_in, cst_in, out):
    with ExitStack() as ctx:
        def sb(name, shape, dt=F32):
            return ctx.enter_context(nc.sbuf_tensor(name, shape, dt))

        def sem(name):
            return ctx.enter_context(nc.semaphore(name))

        x_sb = sb("x_sb", [128, CHUNKS * ALL_ROWS])
        col128, n128 = starts(P128)
        col65, n65 = starts(P65)
        col119, n119 = starts(P119)
        colc, nc_ = starts(CST)
        p128 = sb("p128", [128, n128])
        p65 = sb("p65", [D + 1, n65])
        p119 = sb("p119", [RMAX, n119])
        b2 = sb("b2", [EXPERTS, D])
        cst = sb("cst", [128, nc_])

        def v128(name):
            return p128[:, col128[name][0]:col128[name][1]]

        def v65(name, rows=D):
            return p65[0:rows, col65[name][0]:col65[name][1]]

        def v119(name):
            return p119[:, col119[name][0]:col119[name][1]]

        def const(name, rows=128):
            return cst[0:rows, colc[name][0]:colc[name][1]]

        tokw = v128("tokw").rearrange("p (c e) -> p c e", c=CHUNKS)
        wvT = v128("wvT").rearrange("p (c e) -> p c e", c=2)
        woutbd = v128("woutbd").rearrange("p (c n) -> p c n", c=2)
        w2 = v128("w2").rearrange("p (e d) -> p e d", e=EXPERTS)
        wqk = v65("wqk").rearrange("p (c m) -> p c m", c=4)
        wg = v65("wg", D + 1)
        w1 = v65("w1", D + 1).rearrange("p (e h) -> p e h", e=EXPERTS)
        toep = v119("toep").rearrange("p (h c) -> p h c", h=HEADS)
        ident = const("ident")

        h = sb("h", [RMAX, TILES, D])
        base = sb("base", [RMAX, TILES, D])
        h2 = sb("h2", [RMAX, TILES, D])
        res = sb("res", [RMAX, TILES, D])
        stats = sb("stats", [RMAX, TILES, 6])
        moments = sb("moments", [RMAX, TILES, 2])
        powarg = sb("powarg", [RMAX, TILES, 2])
        rstd = sb("rstd", [RMAX, TILES, 2])
        exponent = sb("exponent", [RMAX, 2])
        xc = sb("xc", [RMAX, TILES, D])
        xnT = sb("xnT", [D, ALL_ROWS])
        qk = sb("qk", [128, 2, 4, RMAX])
        wvo = sb("wvo", [D, HEADS * D])
        v = sb("v", [RMAX, TILES, HEADS * D])
        score = sb("score", [RMAX, 2, HEADS, ROWS])
        smax = sb("smax", [RMAX, 2, HEADS])
        e = sb("e", [RMAX, 2, HEADS, ROWS])
        z = sb("z", [RMAX, 2, HEADS])
        rz = sb("rz", [RMAX, 2, HEADS])
        a = sb("a", [RMAX, TILES, HEADS, ROWS])
        peaks = sb("peaks", [RMAX, 2, TILES])
        colw = sb("colw", [PER_TILE, 3, HEADS, ROWS])
        peak = sb("peak", [RMAX, 2])
        peak2 = sb("peak2", [2, 1])
        peakd = sb("peakd", [2, 2])
        scale = sb("scale", [RMAX, 1])
        rscale = sb("rscale", [RMAX, 1])
        ones2 = sb("ones2", [2, RMAX])
        bd = sb("bd", [RMAX, TILES, 2, HEADS, WIDE], F16)
        bd2 = sb("bd2", [RMAX, TILES, 2, HEADS, WIDE], F16)
        aT = sb("aT", [RMAX, TILES, 2, HEADS, WIDE], F16)
        a16 = sb("a16", [RMAX, TILES, 2, HEADS, ROWS], F16)
        x16 = sb("x16", [RMAX, TILES, 2, HEADS, ROWS], F16)
        x2_16 = sb("x2_16", [RMAX, TILES, 2, HEADS, ROWS], F16)
        w16 = sb("w16", [RMAX, TILES, 2, HEADS, ROWS], F16)
        eye16 = sb("eye16", [RMAX, ROWS], F16)
        blocks16 = sb("blocks16", [RMAX, RMAX], F16)
        ident16 = sb("ident16", [128, 128], F16)
        v3 = sb("v3", [RMAX, TILES, 3, HEADS * D], BF16)
        vrest = sb("vrest", [RMAX, 2, HEADS * D])
        toepbd = sb("toepbd", [RMAX, HEADS, RMAX])
        xm = sb("xm", [RMAX, TILES, HEADS, ROWS])
        xw = sb("xw", [RMAX, TILES, HEADS, ROWS])
        yv3 = sb("yv3", [RMAX, 2, 3, HEADS * D], BF16)
        yvrest = sb("yvrest", [RMAX, 2, HEADS * D])
        farl = sb("farl", [128, RMAX], BF16)
        farr = sb("farr", [128, 2, RMAX], BF16)
        zn = sb("zn", [RMAX, TILES, D])
        zT = sb("zT", [D + 1, TILES, RMAX])
        gate = sb("gate", [RMAX, EXPERTS])
        over = sb("over", [RMAX, EXPERTS, EXPERTS])
        tied = sb("tied", [RMAX, EXPERTS, EXPERTS])
        rank = sb("rank", [RMAX, EXPERTS])
        pick = sb("pick", [RMAX, TILES, EXPERTS])
        pickT = sb("pickT", [EXPERTS, 2, RMAX])
        pickTb = sb("pickTb", [EXPERTS, 2, RMAX], BF16)
        onehot = sb("onehot", [EXPERTS, EXPERTS, HIDDEN], BF16)
        hid = sb("hid", [HIDDEN, 2, EXPERTS, RMAX])
        hidm = sb("hidm", [HIDDEN, 2, EXPERTS, RMAX])

        ps = ctx.enter_context(nc.psum_tensor("ps", [128, 8, 512], F32))

        def bank(b, rows, cols):
            return ps[0:rows, b, 0:cols]

        B_EMB, B_XT, B_QK, B_V, B_SCORE = 0, 1, 2, 3, 4
        def B_GRAM(t): return 0 if t < 3 else 1
        def B_COLS(t): return 2 if t < 3 else 3
        def B_AT(n): return 4 + n % 3
        B_TOEP, B_WVO, B_PEAK = 7, 7, 7
        def B_ITER(t): return 2 + t
        B_YV, B_ATT, B_FFN, B_MISC, B_UP, B_PICK = 0, 1, 2, 3, 4, 6

        def at3(t): return (t if t < 3 else t - 3) * C

        x_in_sem = [sem(f"x_loaded{t}") for t in range(TILES)]
        tokw_loaded, p128_loaded, p65_loaded = sem("tokw_loaded"), sem("p128_loaded"), sem("p65_loaded")
        p119_loaded, cst_loaded, b2_loaded = sem("p119_loaded"), sem("cst_loaded"), sem("b2_loaded")
        stored = sem("stored")
        wvo_done, emb_done, xt_done, qk_done, v_done = (sem(n) for n in (
            "wvo_done", "emb_done", "xt_done", "qk_done", "v_done"))
        score_done, cols_done, gram_done, at_done = (sem(n) for n in (
            "score_done", "cols_done", "gram_done", "at_done"))
        toep_done, peakT_done, peakb_done = sem("toep_done"), sem("peakT_done"), sem("peakb_done")
        x2_done, prod_done = sem("x2_done"), sem("prod_done")
        yv_done, att_done, zt_done, gate_done = (sem(n) for n in ("yv_done", "att_done", "zt_done", "gate_done"))
        up_done, pickT_done, pickb_done, ffn_done = (sem(n) for n in (
            "up_done", "pickT_done", "pickb_done", "ffn_done"))
        dve_step = sem("dve_step")
        setup_done = sem("setup_done")
        emb_read, arg_ready, xc_ready = sem("emb_read"), sem("arg_ready"), sem("xc_ready")
        k_ready, score_ready, score_read = sem("k_ready"), sem("score_ready"), sem("score_read")
        a_ready, abd_ready = sem("a_ready"), sem("abd_ready")
        peak_ready, peakd_ready = sem("peak_ready"), sem("peakd_ready")
        ah_ready = sem("ah_ready")
        al_ready = sem("al_ready")
        x_ready, xbd_ready, w_ready, x2l_ready, x2bd_ready = (sem(n) for n in (
            "x_ready", "xbd_ready", "w_ready", "x2l_ready", "x2bd_ready"))
        xh_ready, x2h_ready, wh_ready = sem("xh_ready"), sem("x2h_ready"), sem("wh_ready")
        xl_ready, wl_ready = sem("xl_ready"), sem("wl_ready")
        x2bd_act_ready = sem("x2bd_act_ready")
        v_cut, v_cut_step = sem("v_cut"), sem("v_cut_step")
        yv1_ready, yvrest_ready, yv2_ready, yv3_ready = (sem(n) for n in (
            "yv1_ready", "yvrest_ready", "yv2_ready", "yv3_ready"))
        h2_read, arg2_ready, zn_ready = sem("h2_read"), sem("arg2_ready"), sem("zn_ready")
        gate_read, pick_ready, pickT_ready, hidm_ready, res_ready = (sem(n) for n in (
            "gate_read", "pick_ready", "pickT_ready", "hidm_ready", "res_ready"))
        wvo_ready, xnT_ready, q_ready, v_ready, e_ready = (sem(n) for n in (
            "wvo_ready", "xnT_ready", "q_ready", "v_ready", "e_ready"))
        at_ready, zT_ready, hid_ready = sem("at_ready"), sem("zT_ready"), sem("hid_ready")
        xbd_act_ready = sem("xbd_act_ready")
        pool_setup, rstd_ready, rstd2_ready, base_ready, base_step = (sem(n) for n in (
            "pool_setup", "rstd_ready", "rstd2_ready", "base_ready", "base_step"))

        def x_tile(t, c):
            at = CHUNKS * OFF[t] + c * R[t]
            return x_sb[:, at:at + R[t]]

        def blocks(t, ap):
            return ap[:, :, None, :].broadcast_to([R[t], ap.shape[1], BLOCKS[t], ROWS])

        def mask(t, heads=HEADS):
            m = const("blocks", R[t])[:, 0:R[t]].rearrange("p (g c) -> p g c", c=ROWS)
            return m[:, None, :, :].broadcast_to([R[t], heads, BLOCKS[t], ROWS])

        def spread(engine_tt, dst, src, t, n):
            r = slice(0, R[t])
            shape = [R[t], 2 * HEADS, n, ROWS]
            m = blocks16[r, 0:n * ROWS].rearrange("p (g c) -> p g c", c=ROWS)
            return engine_tt(
                dst[r, t, :, :, 0:n * ROWS].rearrange("p s h (g c) -> p (s h) g c", c=ROWS),
                src[r, t].rearrange("p s h c -> p (s h) c")[:, :, None, :].broadcast_to(shape),
                m[:, None, :, :].broadcast_to(shape), ALU.mult)

        def by_image(ap):
            return ap.rearrange("p h (g c) -> p h g c", c=ROWS)

        ACT_BLOCKS = 2
        block = ctx.enter_context(nc.Block())

        @block.sync
        def _(sp):
            sp.dma_start(p128[:, 0:CHUNKS * D], p128_in[:, 0:CHUNKS * D]).then_inc(tokw_loaded, 16)
            for t in range(TILES):
                cols = slice(CHUNKS * OFF[t], CHUNKS * (OFF[t] + R[t]))
                sp.dma_start(x_sb[:, cols], x_in[:, cols]).then_inc(x_in_sem[t], 16)
            for t in range(TILES):
                sp.wait_ge(res_ready, t + 1)
                sp.dma_start(out[OFF[t]:OFF[t] + R[t], :], res[0:R[t], t, :]).then_inc(stored, 16)
            sp.wait_ge(stored, 16 * TILES)

        @block.gpsimd
        def _(pool):
            for n, (part, value) in enumerate((
                    (exponent[:], -0.5), (xnT[:], 0.0), (v[64:RMAX, TILES - 1, :], 0.0), (peaks[:], 0.0),
                    (ones2[:], 1.0), (zT[D:D + 1, :, :], 1.0), (base[64:RMAX, TILES - 1, :], 0.0),
                    *((m[:, 0:TILES - 1, :, :, RMAX:], 0.0) for m in (bd, bd2, aT)),
                    *((m[:, TILES - 1, :, :, R[-1]:], 0.0) for m in (bd, bd2, aT)))):
                if n:
                    pool.wait_ge(pool_setup, n)
                nc.gpsimd.memset(part, value).then_inc(pool_setup, 1)
            pool.wait_ge(pool_setup, 13)
            pool.wait_ge(p119_loaded, 16)
            for t in range(TILES):
                r = slice(0, R[t])
                pool.wait_ge(arg_ready, 2 * (t + 1))
                nc.gpsimd.tensor_tensor(rstd[r, t, :], powarg[r, t, :], exponent[r, :],
                                        ALU.pow).then_inc(rstd_ready, 1)
            for t in range(TILES):
                r = slice(0, R[t])
                pool.wait_ge(xc_ready, 2 * (t + 1))
                nc.gpsimd.tensor_tensor(base[r, t, :], h[r, t, :], v119("bout")[r, :],
                                        ALU.add).then_inc(base_step, 1)
                pool.wait_ge(base_step, t + 1)
                nc.gpsimd.tensor_tensor(base[r, t, :], base[r, t, :], h2[r, t, :],
                                        ALU.add).then_inc(base_ready, 1)
            for t in range(TILES):
                r = slice(0, R[t])
                pool.wait_ge(v_ready, t + 1)
                nc.gpsimd.tensor_copy(v3[r, t, 0], v[r, t]).then_inc(v_cut_step, 1)
                pool.wait_ge(v_cut_step, 3 * t + 1)
                nc.gpsimd.tensor_tensor(vrest[r, t % 2], v[r, t], v3[r, t, 0], ALU.subtract).then_inc(v_cut_step, 1)
                pool.wait_ge(v_cut_step, 3 * t + 2)
                nc.gpsimd.tensor_copy(v3[r, t, 1], vrest[r, t % 2]).then_inc(v_cut_step, 1)
                pool.wait_ge(v_cut_step, 3 * t + 3)
                nc.gpsimd.tensor_tensor(v3[r, t, 2], vrest[r, t % 2], v3[r, t, 1], ALU.subtract).then_inc(v_cut, 1)

            def second_x(t, count):
                pool.wait_ge(xh_ready, count)
                nc.gpsimd.tensor_tensor(x16[0:R[t], t, 1], xm[0:R[t], t], x16[0:R[t], t, 0], ALU.subtract
                                        ).then_inc(xl_ready, 1)

            for t in range(TILES):
                second_x(t, t + 1)
            with pool.Fori(0, ITERS) as it:
                for t in range(TILES):
                    pool.wait_ge(wh_ready, it * TILES + (t + 1))
                    nc.gpsimd.tensor_tensor(w16[0:R[t], t, 1], xw[0:R[t], t], w16[0:R[t], t, 0], ALU.subtract
                                            ).then_inc(wl_ready, 1)
                for t in range(TILES):
                    second_x(t, it * TILES + (TILES + t + 1))
            for t in range(TILES):
                r = slice(0, R[t])
                pool.wait_ge(arg2_ready, t + 1)
                nc.gpsimd.tensor_tensor(rstd[r, t, 0:1], powarg[r, t, 0:1], exponent[r, 0:1],
                                        ALU.pow).then_inc(rstd2_ready, 1)

        @block.scalar
        def _(act):
            act.dma_start(cst[:, :], cst_in).then_inc(cst_loaded, 16)
            act.dma_start(p119[:, :], p119_in).then_inc(p119_loaded, 16)
            act.dma_start(p65[:, :], p65_in).then_inc(p65_loaded, 16)
            act.dma_start(p128[:, CHUNKS * D:], p128_in[:, CHUNKS * D:]).then_inc(p128_loaded, 16)
            act.dma_start(b2[:, :], b2_in).then_inc(b2_loaded, 16)
            act.wait_ge(wvo_done, 1)
            nc.scalar.copy(wvo[:, :], bank(B_WVO, D, HEADS * D)).then_inc(wvo_ready, 1)

            def softmax_exp(t):
                act.wait_ge(score_ready, t + 1)
                nc.scalar.activation(e[0:R[t], t % 2], score[0:R[t], t % 2], ACT.Exp).then_inc(e_ready, 1)

            def first_a(t):
                act.wait_ge(a_ready, 2 * t + 1)
                nc.scalar.copy(a16[0:R[t], t, 0], a[0:R[t], t]).then_inc(ah_ready, 1)

            act.wait_ge(p65_loaded, 16)
            act.wait_ge(pool_setup, 13)
            ln = v65("ln")
            for t in range(TILES + 1):
                if t >= 2:
                    first_a(t - 2)
                if t < TILES:
                    r = slice(0, R[t])
                    act.wait_ge(xt_done, t + 1)
                    cols = slice(OFF[t], OFF[t] + R[t])
                    nc.scalar.activation(
                        xnT[:, cols].rearrange("p (n s) -> p n s", s=ROWS)[:, :, 1:ROWS],
                        bank(B_XT, D, R[t]).rearrange("p (n s) -> p n s", s=ROWS)[:, :, 1:ROWS],
                        ACT.Identity, bias=ln[:, 1:2], scale=ln[:, 0:1]).then_inc(xnT_ready, 1)
                    act.wait_ge(qk_done, t + 1)
                    if t >= 2:
                        act.wait_ge(score_done, 4 * (t - 1))
                    nc.scalar.activation(qk[:, t % 2, 0:2, 0:R[t]],
                                         bank(B_QK, 128, 2 * R[t]).rearrange("p (c n) -> p c n", c=2),
                                         ACT.Copy, scale=DH ** -0.5).then_inc(q_ready, 1)
                    nc.scalar.activation(qk[:, t % 2, 2:4, 0:R[t]],
                                         ps[:, B_QK, 2 * R[t]:4 * R[t]].rearrange("p (c n) -> p c n", c=2),
                                         ACT.Copy).then_inc(q_ready, 1)
                    act.wait_ge(v_done, t + 1)
                    nc.scalar.copy(v[r, t, :], bank(B_V, R[t], HEADS * D)).then_inc(v_ready, 1)
                if t >= 1:
                    softmax_exp(t - 1)
            first_a(TILES - 1)
            for n in range(2 * TILES):
                t, part = n // 2, n % 2
                act.wait_ge(at_done, n + 1)
                nc.scalar.copy(aT[0:R[t], t, part, :, 0:R[t]],
                               ps[0:R[t], B_AT(n), :].bitcast(F16).rearrange("p (h n) -> p h n", h=HEADS)[:, :, 0:R[t]]
                               ).then_inc(at_ready, 1)

            def spread_last(dst, src, t):
                r = slice(0, R[t])
                for g in range(BLOCKS[t] - ACT_BLOCKS, BLOCKS[t]):
                    last = nc.scalar.activation(
                        dst[r, t, :, :, ROWS * g:ROWS * g + ROWS].rearrange("p s h c -> p (s h) c"),
                        src[r, t].rearrange("p s h c -> p (s h) c"), ACT.Copy,
                        scale=const("blocks", R[t])[:, ROWS * g:ROWS * g + 1])
                return last

            def first_x(t, count):
                act.wait_ge(x_ready, count)
                nc.scalar.copy(x16[0:R[t], t, 0], xm[0:R[t], t]).then_inc(xh_ready, 1)

            def spread_x(t, count):
                act.wait_ge(xl_ready, count)
                spread_last(bd, x16, t).then_inc(xbd_act_ready, 1)

            def first_x2_w(t, count):
                r = slice(0, R[t])
                act.wait_ge(w_ready, count)
                nc.scalar.activation(x2_16[r, t, 0], ps[r, B_ITER(t), 0:C].rearrange("p (h c) -> p h c", c=ROWS),
                                     ACT.Copy, scale=-1.0 / 7.0).then_inc(x2h_ready, 1)
                nc.scalar.copy(w16[r, t, 0], xw[r, t]).then_inc(wh_ready, 1)

            def spread_x2(t, count):
                act.wait_ge(x2l_ready, count)
                spread_last(bd2, x2_16, t).then_inc(x2bd_act_ready, 1)

            act.wait_ge(at_done, 2 * TILES)
            act.wait_ge(gram_done, TILES)
            for t in range(TILES):
                first_x(t, t + 1)
                if t >= 1:
                    spread_x(t - 1, t)
            with act.Fori(0, ITERS) as it:
                for t in range(TILES):
                    first_x2_w(t, it * TILES + (t + 1))
                    if t == 0:
                        spread_x(TILES - 1, it * TILES + TILES)
                    else:
                        spread_x2(t - 1, it * TILES + t)
                for t in range(TILES):
                    first_x(t, it * TILES + (TILES + t + 1))
                    if t == 0:
                        spread_x2(TILES - 1, it * TILES + TILES)
                    else:
                        spread_x(t - 1, it * TILES + (TILES + t))
            spread_x(TILES - 1, (ITERS + 1) * TILES)

            for s in range(TILES + 1):
                if s < TILES:
                    act.wait_ge(yv_done, s + 1)
                    if s >= 2:
                        act.wait_ge(att_done, s - 1)
                    nc.scalar.activation(yv3[0:R[s], s % 2, 0], bank(B_YV, R[s], HEADS * D), ACT.Copy,
                                         scale=1.0 / ALPHA).then_inc(yv1_ready, 1)
                    act.wait_ge(yvrest_ready, s + 1)
                    nc.scalar.copy(yv3[0:R[s], s % 2, 1], yvrest[0:R[s], s % 2]).then_inc(yv2_ready, 1)
                if s >= 1:
                    t = s - 1
                    for half in range(2):
                        act.wait_ge(up_done, 2 * t + half + 1)
                        if t >= 2 and half == 0:
                            act.wait_ge(hidm_ready, 2 * (t - 1))
                        nc.scalar.activation(hid[:, t % 2, 4 * half:4 * half + 4, 0:R[t]],
                                             bank(B_UP + half, HIDDEN, 4 * R[t]).rearrange(
                                                 "p (e n) -> p e n", e=4),
                                             ACT.Gelu).then_inc(hid_ready, 1)
                if s < TILES:
                    act.wait_ge(zt_done, s + 1)
                    nc.scalar.copy(zT[0:D, s, 0:R[s]], bank(B_MISC, D, R[s])).then_inc(zT_ready, 1)

        @block.vector
        def _(dve):
            steps = [0]

            def own(instruction):
                steps[0] += 1
                instruction.then_inc(dve_step, 1)
                dve.wait_ge(dve_step, steps[0])

            tt, ts, stt = nc.vector.tensor_tensor, nc.vector.tensor_scalar, nc.vector.scalar_tensor_tensor
            dve.wait_ge(cst_loaded, 16)
            nc.vector.tensor_copy(farl[:, :], const("farl")).then_inc(setup_done, 1)
            nc.vector.tensor_copy(farr[:, :, :], const("farr").rearrange("p (a n) -> p a n", a=2)
                                  ).then_inc(setup_done, 1)
            nc.vector.tensor_copy(onehot[:, :, :],
                                  ident[0:EXPERTS, 0:EXPERTS][:, :, None].broadcast_to(
                                      [EXPERTS, EXPERTS, HIDDEN])).then_inc(setup_done, 1)
            nc.vector.tensor_copy(eye16[:, :], const("eye", RMAX)).then_inc(setup_done, 1)
            nc.vector.tensor_copy(blocks16[:, :], const("blocks", RMAX)).then_inc(setup_done, 1)
            nc.vector.tensor_copy(ident16[:, :], ident).then_inc(setup_done, 1)
            dve.wait_ge(p119_loaded, 16)
            tt(by_image(toepbd[:, :, :]), blocks(0, toep), mask(0), ALU.mult).then_inc(setup_done, 1)

            def layernorm_stats(t, src):
                r = slice(0, R[t])
                own(nc.vector.bn_stats(stats[r, t, :], src))
                own(nc.vector.bn_aggr(moments[r, t, :], stats[r, t, :]))

            def embed(t):
                r = slice(0, R[t])
                dve.wait_ge(emb_done, t + 1)
                tt(h[r, t, :], bank(B_EMB, R[t], D), v119("tokb")[r, :], ALU.add).then_inc(emb_read, 1)
                dve.wait_ge(emb_read, t + 1)
                layernorm_stats(t, h[r, t, :])
                ts(powarg[r, t, 0:1], moments[r, t, 1:2], EPS, None, ALU.add).then_inc(arg_ready, 1)
                ts(powarg[r, t, 1:2], moments[r, t, 1:2], 1.0 + EPS, EPS * EPS, ALU.mult, ALU.add
                   ).then_inc(arg_ready, 1)

            def normalise(t):
                r = slice(0, R[t])
                dve.wait_ge(rstd_ready, t + 1)
                ts(xc[r, t, :], h[r, t, :], moments[r, t, 0:1], rstd[r, t, 1:2], ALU.subtract, ALU.mult
                   ).then_inc(xc_ready, 1)
                ts(h2[r, t, :], h[r, t, :], moments[r, t, 0:1], rstd[r, t, 0:1], ALU.subtract, ALU.mult
                   ).then_inc(xc_ready, 1)

            def scores_out(t):
                r = slice(0, R[t])
                p = t % 2
                if t >= 2:
                    dve.wait_ge(e_ready, t - 1)
                for j in range(4):
                    dve.wait_ge(score_done, 4 * t + j + 1)
                    nc.vector.tensor_reduce(
                        score[r, p, j:HEADS:4, :],
                        bank(B_SCORE + j, R[t], 2 * R[t]).rearrange("p (a g c) -> p a c g", a=2, c=ROWS),
                        AX, ALU.max).then_inc(score_read, 1)
                dve.wait_ge(score_read, 4 * (t + 1))
                own(nc.vector.tensor_reduce(smax[r, p, :], score[r, p], AX, ALU.max))
                tt(score[r, p], score[r, p], smax[r, p, :, None].broadcast_to([R[t], HEADS, ROWS]),
                   ALU.subtract).then_inc(score_ready, 1)

            def softmax(t):
                r = slice(0, R[t])
                p = t % 2
                wcol = const("wcol", R[t])[:, None, :].broadcast_to([R[t], HEADS, ROWS])
                wsym = const("wsym", R[t])[:, None, :].broadcast_to([R[t], HEADS, ROWS])
                dve.wait_ge(e_ready, t + 1)
                own(tt(e[r, p], e[r, p], wcol, ALU.mult))
                own(nc.vector.tensor_reduce(z[r, p, :], e[r, p], AX, ALU.add))
                own(nc.vector.reciprocal(rz[r, p, :], z[r, p, :]))
                own(tt(e[r, p], e[r, p], rz[r, p, :, None].broadcast_to([R[t], HEADS, ROWS]), ALU.mult))
                tt(a[r, t], e[r, p], wsym, ALU.mult).then_inc(a_ready, 1)
                own(nc.vector.tensor_reduce(z[r, p, :], e[r, p], AX, ALU.add))
                nc.vector.tensor_reduce(peaks[r, 0, t:t + 1], z[r, p, :], AX, ALU.max).then_inc(a_ready, 1)
                if t == 0:
                    dve.wait_ge(setup_done, 7)
                dve.wait_ge(ah_ready, t + 1)
                dve.wait_ge(a_ready, 2 * t + 1)
                tt(a16[r, t, 1], a[r, t], a16[r, t, 0], ALU.subtract).then_inc(al_ready, 1)
                dve.wait_ge(al_ready, t + 1)
                spread(tt, bd, a16, t, BLOCKS[t]).then_inc(abd_ready, 1)

            for t in range(TILES + 2):
                if t < TILES:
                    embed(t)
                if 1 <= t <= TILES:
                    normalise(t - 1)
                if t >= 2:
                    scores_out(t - 2)
                if t >= 2:
                    if t == 2:
                        dve.wait_ge(pool_setup, 7)
                    softmax(t - 2)

            def column_peaks(tiles, rows, count):
                dve.wait_ge(cols_done, count)
                n = len(tiles)
                t0 = tiles[0]
                own(tt(colw[0:rows, 0:n].rearrange("p t h c -> p (t h) c"),
                       ps[0:rows, B_COLS(t0), at3(t0):at3(t0) + n * C].rearrange("p (h c) -> p h c", c=ROWS),
                       const("winv", rows)[:, None, :].broadcast_to([rows, n * HEADS, ROWS]), ALU.mult))
                own(nc.vector.tensor_reduce(peaks[0:rows, 1, t0:t0 + n],
                                            colw[0:rows, 0:n].rearrange("p t h c -> p t (h c)"),
                                            AX, ALU.max))

            dve.wait_ge(a_ready, 2 * TILES)
            column_peaks([0, 1, 2], PER_TILE, 3)
            column_peaks([3], PER_TILE, TILES)
            column_peaks([4], BLOCKS[4], TILES)
            nc.vector.tensor_reduce(peak[:, :], peaks[:, :, :], AX, ALU.max).then_inc(peak_ready, 1)
            dve.wait_ge(peakT_done, 1)
            own(nc.vector.tensor_reduce(peak2[:, :], bank(B_PEAK, 2, RMAX), AX, ALU.max))
            ts(peakd[:, :], ident[0:2, 0:2], peak2[:, 0:1], None, ALU.mult).then_inc(peakd_ready, 1)
            dve.wait_ge(peakb_done, 1)
            own(nc.vector.tensor_reduce(scale[:, :], bank(B_PEAK, RMAX, 2), AX, ALU.mult))
            own(nc.vector.reciprocal(rscale[:, :], scale[:, :]))

            def new_x(t, count):
                r = slice(0, R[t])
                prod = ps[r, B_ITER(t), C:2 * C].rearrange("p (h c) -> p h c", c=ROWS)
                dve.wait_ge(prod_done, count)
                stt(xm[r, t], xm[r, t], 13.0 / 4.0, prod, ALU.mult, ALU.add).then_inc(x_ready, 1)

            def spread_x(t, count):
                dve.wait_ge(xl_ready, count)
                spread(tt, bd, x16, t, BLOCKS[t] - ACT_BLOCKS).then_inc(xbd_ready, 1)

            def new_w(t, count):
                r = slice(0, R[t])
                dve.wait_ge(x2_done, count)
                stt(xw[r, t], ps[r, B_ITER(t), 0:C].rearrange("p (h c) -> p h c", c=ROWS), 2.0 / 49.0, xm[r, t],
                    ALU.mult, ALU.subtract).then_inc(w_ready, 1)

            def second_x2(t, count):
                r = slice(0, R[t])
                dve.wait_ge(x2h_ready, count)
                stt(x2_16[r, t, 1], ps[r, B_ITER(t), 0:C].rearrange("p (h c) -> p h c", c=ROWS), -1.0 / 7.0,
                    x2_16[r, t, 0], ALU.mult, ALU.subtract).then_inc(x2l_ready, 1)

            def spread_x2(t, count):
                dve.wait_ge(x2l_ready, count)
                spread(tt, bd2, x2_16, t, BLOCKS[t] - ACT_BLOCKS).then_inc(x2bd_ready, 1)

            dve.wait_ge(gram_done, TILES)
            dve.wait_ge(at_done, 2 * TILES)
            for t in range(TILES):
                r = slice(0, R[t])
                ts(xm[r, t].rearrange("p h c -> p (h c)"), ps[r, B_GRAM(t), at3(t):at3(t) + C],
                   rscale[r, 0:1], ALPHA, ALU.mult, ALU.mult).then_inc(x_ready, 1)
                if t >= 1:
                    spread_x(t - 1, t)
            with dve.Fori(0, ITERS) as it:
                for t in range(TILES):
                    new_w(t, it * TILES + (t + 1))
                    if t == 0:
                        spread_x(TILES - 1, it * TILES + TILES)
                    else:
                        second_x2(t - 1, it * TILES + t)
                        spread_x2(t - 1, it * TILES + t)
                for t in range(TILES):
                    if t == 0:
                        second_x2(TILES - 1, it * TILES + TILES)
                    new_x(t, it * TILES + (t + 1))
                    if t == 0:
                        spread_x2(TILES - 1, it * TILES + TILES)
                    else:
                        spread_x(t - 1, it * TILES + (TILES + t))
            spread_x(TILES - 1, (ITERS + 1) * TILES)
            dve.wait_ge(toep_done, 1)
            dve.wait_ge(base_ready, TILES)
            own(tt(base[:, :, :], base[:, :, :],
                   bank(B_TOEP, RMAX, TILES * D).rearrange("p (t d) -> p t d", t=TILES), ALU.add))

            def rest_of_yv(t):
                r = slice(0, R[t])
                p = t % 2
                dve.wait_ge(yv1_ready, t + 1)
                stt(yvrest[r, p], bank(B_YV, R[t], HEADS * D), 1.0 / ALPHA, yv3[r, p, 0], ALU.mult, ALU.subtract
                    ).then_inc(yvrest_ready, 1)
                dve.wait_ge(yv2_ready, t + 1)
                tt(yv3[r, p, 2], yvrest[r, p], yv3[r, p, 1], ALU.subtract).then_inc(yv3_ready, 1)

            def attention_out(t):
                r = slice(0, R[t])
                dve.wait_ge(att_done, t + 1)
                tt(h2[r, t, :], base[r, t, :], bank(B_ATT, R[t], D), ALU.add).then_inc(h2_read, 1)
                dve.wait_ge(h2_read, t + 1)
                layernorm_stats(t, h2[r, t, :])
                ts(powarg[r, t, 0:1], moments[r, t, 1:2], EPS, None, ALU.add).then_inc(arg2_ready, 1)
                dve.wait_ge(rstd2_ready, t + 1)
                ts(zn[r, t, :], h2[r, t, :], moments[r, t, 0:1], rstd[r, t, 0:1], ALU.subtract, ALU.mult
                   ).then_inc(zn_ready, 1)

            def choose(t):
                r = slice(0, R[t])
                shape = [R[t], EXPERTS, EXPERTS]
                dve.wait_ge(gate_done, t + 1)
                nc.vector.tensor_copy(gate[r, :], bank(B_MISC, R[t], EXPERTS)).then_inc(gate_read, 1)
                dve.wait_ge(gate_read, t + 1)
                other = gate[r, None, :].broadcast_to(shape)
                mine = gate[r, :, None].broadcast_to(shape)
                own(tt(tied[r], other, mine, ALU.is_equal))
                own(tt(over[r], other, mine, ALU.is_gt))
                own(tt(tied[r], tied[r], const("before", R[t]).rearrange("p (e j) -> p e j", e=EXPERTS), ALU.mult))
                own(tt(over[r], over[r], tied[r], ALU.add))
                own(nc.vector.tensor_reduce(rank[r, :], over[r], AX, ALU.add))
                ts(pick[r, t, :], rank[r, :], 2.0, None, ALU.is_lt).then_inc(pick_ready, 1)

            def pick_out(t):
                p = t % 2
                dve.wait_ge(pickT_done, t + 1)
                if t >= 2:
                    dve.wait_ge(ffn_done, t - 1)
                src = bank(B_MISC, EXPERTS, R[t])
                nc.vector.tensor_copy(pickT[:, p, 0:R[t]], src).then_inc(pickT_ready, 1)
                nc.vector.tensor_copy(pickTb[:, p, 0:R[t]], src).then_inc(pickT_ready, 1)

            def pick_hidden(t, half):
                p = t % 2
                dve.wait_ge(pickb_done, 2 * t + half + 1)
                dve.wait_ge(hid_ready, 2 * t + half + 1)
                tt(hidm[:, p, 4 * half:4 * half + 4, 0:R[t]], hid[:, p, 4 * half:4 * half + 4, 0:R[t]],
                   bank(B_PICK + half, HIDDEN, 4 * R[t]).rearrange("p (e n) -> p e n", e=4), ALU.mult
                   ).then_inc(hidm_ready, 1)

            def result(t):
                r = slice(0, R[t])
                dve.wait_ge(ffn_done, t + 1)
                tt(res[r, t, :], h2[r, t, :], bank(B_FFN, R[t], D), ALU.add).then_inc(res_ready, 1)

            for s in range(TILES + 1):
                if s < TILES:
                    rest_of_yv(s)
                if s >= 1:
                    choose(s - 1)
                if s < TILES:
                    attention_out(s)
                if s >= 1:
                    pick_out(s - 1)
                    pick_hidden(s - 1, 0)
                    pick_hidden(s - 1, 1)
                    result(s - 1)

        @block.tensor
        def _(pe):
            mm = nc.tensor.matmul

            def parts_product(out, stationary, moving, more=()):
                steps = [(stationary[:, i], moving[:, j]) for i in range(stationary.shape[1])
                         for j in range(moving.shape[1])] + list(more)
                for i, (lhsT, rhs) in enumerate(steps):
                    last = mm(out, lhsT, rhs, start=(i == 0), stop=(i == len(steps) - 1))
                return last

            pe.wait_ge(p128_loaded, 16)
            for c in range(2):
                last = mm(ps[0:D, B_WVO, c * 4 * D:(c + 1) * 4 * D], wvT[:, c, :], woutbd[:, c, :],
                          start=True, stop=True)
            last.then_inc(wvo_done, 1)

            def embed(t):
                pe.wait_ge(x_in_sem[t], 16)
                if t == 0:
                    pe.wait_ge(tokw_loaded, 16)
                if t >= 1:
                    pe.wait_ge(emb_read, t)
                for c in range(CHUNKS):
                    last = mm(bank(B_EMB, R[t], D), x_tile(t, c), tokw[:, c, :],
                              start=(c == 0), stop=(c == CHUNKS - 1))
                last.then_inc(emb_done, 1)

            def turn(t):
                pe.wait_ge(xc_ready, 2 * t + 1)
                if t == 0:
                    pe.wait_ge(cst_loaded, 16)
                if t >= 1:
                    pe.wait_ge(xnT_ready, t)
                nc.tensor.transpose(bank(B_XT, D, R[t]), xc[0:R[t], t, :], ident[0:R[t], 0:R[t]]
                                    ).then_inc(xt_done, 1)

            def project(t):
                cols = xnT[:, OFF[t]:OFF[t] + R[t]]
                pe.wait_ge(xnT_ready, t + 1)
                if t == 0:
                    pe.wait_ge(p65_loaded, 16)
                    pe.wait_ge(pool_setup, 13)
                if t >= 1:
                    pe.wait_ge(q_ready, 2 * t)
                for c in range(4):
                    last = mm(ps[:, B_QK, c * R[t]:(c + 1) * R[t]], wqk[:, c, :], cols, start=True, stop=True)
                last.then_inc(qk_done, 1)
                if t == 0:
                    pe.wait_ge(wvo_ready, 1)
                if t >= 1:
                    pe.wait_ge(v_ready, t)
                mm(bank(B_V, R[t], HEADS * D), cols, wvo[:, :], start=True, stop=True).then_inc(v_done, 1)

            def scores(t):
                p = t % 2
                pe.wait_ge(q_ready, 2 * (t + 1))
                if t == 0:
                    pe.wait_ge(setup_done, 2)
                    pe.wait_ge(wvo_ready, 1)
                for j in range(4):
                    if t >= 1:
                        pe.wait_ge(score_read, 4 * (t - 1) + j + 1)
                    g = slice(32 * j, 32 * j + 1 + BLOCKS[t])
                    q = slice(32 * j, 32 * j + 32)
                    mm(bank(B_SCORE + j, R[t], 2 * R[t]).rearrange("p (a n) -> p a n", a=2),
                       farl[g, 0:R[t]], farr[g, :, 0:R[t]], start=True, stop=False, skip_group_check=True)
                    for half in range(2):
                        last = mm(ps[0:R[t], B_SCORE + j, half * R[t]:(half + 1) * R[t]],
                                  qk[q, p, half, 0:R[t]], qk[q, p, 2 + half, 0:R[t]],
                                  start=False, stop=True, skip_group_check=True)
                    last.then_inc(score_done, 1)

            def gram(t):
                r = slice(0, R[t])
                pe.wait_ge(a_ready, 2 * t + 1)
                mm(ps[0:BLOCKS[t], B_COLS(t), at3(t):at3(t) + C], const("selw", R[t])[:, 0:BLOCKS[t]],
                   a[r, t].rearrange("p h c -> p (h c)"), start=True, stop=True).then_inc(cols_done, 1)
                pe.wait_ge(abd_ready, t + 1)
                for k in range(HEADS):
                    at = at3(t) + k * ROWS
                    last = parts_product(ps[:, B_GRAM(t), at:at + ROWS], bd[r, t, :, k], a16[r, t, :, k])
                last.then_inc(gram_done, 1)

            def turn_a(n):
                t, part = n // 2, n % 2
                r = slice(0, R[t])
                if n >= 3:
                    pe.wait_ge(at_ready, n - 2)
                out16 = ps[:, B_AT(n), :].bitcast(F16).rearrange("p (h n) -> p h n", h=HEADS)
                for k in range(HEADS):
                    last = nc.tensor.transpose(out16[:, k, 0:R[t]], bd[r, t, part, k, :], ident16[r, r])
                last.then_inc(at_done, 1)

            for s in range(TILES + 2):
                if s < TILES:
                    embed(s)
                if 1 <= s <= TILES:
                    turn(s - 1)
                if s >= 2:
                    scores(s - 2)
                if 1 <= s <= TILES:
                    project(s - 1)

            pe.wait_ge(emb_read, TILES)
            pe.wait_ge(xnT_ready, TILES)
            pe.wait_ge(q_ready, 2 * TILES)
            pe.wait_ge(v_ready, TILES)
            for t in range(TILES):
                gram(t)
                if t == 0:
                    pe.wait_ge(score_read, 4 * TILES)
                turn_a(2 * t)
                turn_a(2 * t + 1)
            pe.wait_ge(peak_ready, 1)
            nc.tensor.transpose(bank(B_PEAK, 2, RMAX), peak[:, :], ident[0:RMAX, 0:RMAX]
                                ).then_inc(peakT_done, 1)
            pe.wait_ge(peakd_ready, 1)
            mm(bank(B_PEAK, RMAX, 2), ones2[:, :], peakd[:, :], start=True, stop=True).then_inc(peakb_done, 1)
            pe.wait_ge(at_ready, 2 * TILES)

            with pe.Fori(0, ITERS) as it:
                for t in range(TILES):
                    r = slice(0, R[t])
                    pe.wait_ge(xbd_ready, it * TILES + (t + 1))
                    pe.wait_ge(xbd_act_ready, it * TILES + (t + 1))
                    for k in range(HEADS):
                        last = parts_product(ps[:, B_ITER(t), k * ROWS:(k + 1) * ROWS],
                                             bd[r, t, :, k], x16[r, t, :, k])
                    last.then_inc(x2_done, 1)
                for t in range(TILES):
                    r = slice(0, R[t])
                    pe.wait_ge(wl_ready, it * TILES + (t + 1))
                    pe.wait_ge(x2bd_ready, it * TILES + (t + 1))
                    pe.wait_ge(x2bd_act_ready, it * TILES + (t + 1))
                    for k in range(HEADS):
                        last = parts_product(ps[:, B_ITER(t), C + k * ROWS:C + (k + 1) * ROWS],
                                             bd2[r, t, :, k], w16[r, t, :, k],
                                             [(bd2[r, t, i, k], eye16[r, :]) for i in range(2)])
                    last.then_inc(prod_done, 1)

            pe.wait_ge(setup_done, 7)
            for k in range(HEADS):
                last = mm(bank(B_TOEP, RMAX, TILES * D).rearrange("p (t d) -> p t d", t=TILES),
                          toepbd[:, k, :], v[:, :, k * D:(k + 1) * D], start=(k == 0), stop=(k == HEADS - 1))
            last.then_inc(toep_done, 1)

            def x_times_v(t):
                r = slice(0, R[t])
                pe.wait_ge(xbd_ready, TILES * ITERS + t + 1)
                pe.wait_ge(xbd_act_ready, TILES * ITERS + t + 1)
                pe.wait_ge(v_cut, t + 1)
                if t >= 1:
                    pe.wait_ge(yvrest_ready, t)
                for k in range(HEADS):
                    last = parts_product(ps[:, B_YV, k * D:(k + 1) * D], bd[r, t, :, k],
                                         v3[r, t, :, k * D:(k + 1) * D])
                last.then_inc(yv_done, 1)

            def a_times(t):
                r = slice(0, R[t])
                pe.wait_ge(yv3_ready, t + 1)
                if t >= 1:
                    pe.wait_ge(h2_read, t)
                steps = [(k, i, j) for k in range(HEADS) for i in range(2) for j in range(3)]
                for n, (k, i, j) in enumerate(steps):
                    last = mm(bank(B_ATT, 128, D), aT[r, t, i, k], yv3[r, t % 2, j, k * D:(k + 1) * D],
                              start=(n == 0), stop=(n == len(steps) - 1))
                last.then_inc(att_done, 1)

            def turn_z(t):
                pe.wait_ge(zn_ready, t + 1)
                if t >= 1:
                    pe.wait_ge(pickT_ready, 2 * t)
                nc.tensor.transpose(bank(B_MISC, D, R[t]), zn[0:R[t], t, :], ident[0:R[t], 0:R[t]]
                                    ).then_inc(zt_done, 1)

            def gates(t):
                pe.wait_ge(zT_ready, t + 1)
                mm(bank(B_MISC, R[t], EXPERTS), zT[:, t, 0:R[t]], wg, start=True, stop=True
                   ).then_inc(gate_done, 1)

            def up(t):
                for half in range(2):
                    if t >= 1:
                        pe.wait_ge(hid_ready, 2 * (t - 1) + half + 1)
                    for k in range(4):
                        last = mm(ps[:, B_UP + half, k * R[t]:(k + 1) * R[t]], w1[:, 4 * half + k, :],
                                  zT[:, t, 0:R[t]], start=True, stop=True)
                    last.then_inc(up_done, 1)

            def picks(t):
                pe.wait_ge(pick_ready, t + 1)
                nc.tensor.transpose(bank(B_MISC, EXPERTS, R[t]), pick[0:R[t], t, :], ident[0:R[t], 0:R[t]]
                                    ).then_inc(pickT_done, 1)
                pe.wait_ge(pickT_ready, 2 * (t + 1))
                for half in range(2):
                    if t >= 1:
                        pe.wait_ge(hidm_ready, 2 * (t - 1) + half + 1)
                    for k in range(4):
                        last = mm(ps[:, B_PICK + half, k * R[t]:(k + 1) * R[t]], onehot[:, 4 * half + k, :],
                                  pickTb[:, t % 2, 0:R[t]], start=True, stop=True)
                    last.then_inc(pickb_done, 1)

            def down(t):
                if t == 0:
                    pe.wait_ge(b2_loaded, 16)
                if t >= 1:
                    pe.wait_ge(res_ready, t)
                mm(bank(B_FFN, R[t], D), pickT[:, t % 2, 0:R[t]], b2[:, :], start=True, stop=False)
                for k in range(EXPERTS):
                    if k % 4 == 0:
                        pe.wait_ge(hidm_ready, 2 * t + k // 4 + 1)
                    last = mm(bank(B_FFN, R[t], D), hidm[:, t % 2, k, 0:R[t]], w2[:, k, :],
                              start=False, stop=(k == EXPERTS - 1))
                last.then_inc(ffn_done, 1)

            for s in range(TILES + 1):
                if s < TILES:
                    x_times_v(s)
                if s >= 1:
                    gates(s - 1)
                    up(s - 1)
                if s < TILES:
                    a_times(s)
                if s >= 1:
                    picks(s - 1)
                    down(s - 1)
                if s < TILES:
                    turn_z(s)


def shape_constants():
    row = np.arange(RMAX)
    image, place = row // ROWS, row % ROWS
    w = np.where(place == 0, np.sqrt(PADS), 1.0)
    wc = np.where(np.arange(ROWS) == 0, np.sqrt(PADS), 1.0)
    parts = {}
    parts["ident"] = np.eye(128)
    parts["blocks"] = image[:, None] == image[None, :]
    parts["wcol"] = np.broadcast_to(wc * wc, (RMAX, ROWS))
    parts["wsym"] = w[:, None] / wc[None, :]
    parts["eye"] = 15.0 / 2.0 * (place[:, None] == np.arange(ROWS))
    parts["selw"] = w[:, None] * (image[:, None] == np.arange(PER_TILE))
    parts["winv"] = np.broadcast_to(1.0 / wc, (RMAX, ROWS))
    parts["before"] = np.broadcast_to(np.tril(np.ones((EXPERTS, EXPERTS)), -1).reshape(1, -1), (RMAX, EXPERTS ** 2))
    farl, farr = np.zeros((128, RMAX)), np.zeros((128, 2, RMAX))
    for j in range(4):
        farl[32 * j] = -FAR
        farr[32 * j] = 1.0
        for g in range(PER_TILE):
            farl[32 * j + 1 + g] = FAR * (image == g)
            farr[32 * j + 1 + g] = image == g
    parts["farl"], parts["farr"] = farl, farr.reshape(128, -1)
    cols, n = starts(CST)
    out = np.zeros((128, n), np.float32)
    for name, (lo, hi) in cols.items():
        out[:len(parts[name]), lo:hi] = parts[name]
    return out


def pack(rows, widths, parts):
    cols, n = starts(widths)
    out = np.zeros((rows, n), np.float32)
    for name, (lo, hi) in cols.items():
        out[:len(parts[name]), lo:hi] = parts[name]
    return out


def kernel(x, L0_tok_W, L0_tok_b, L0_attn_ln_g, L0_attn_ln_b, L0_attn_w_qkv, L0_attn_w_out, L0_attn_b_out,
           L0_attn_res_kernel, L0_ffn_Wg, L0_ffn_bg, L0_ffn_W1, L0_ffn_b1, L0_ffn_W2, L0_ffn_b2):
    import concourse.bacc as bacc
    from concourse.bass_utils import run_bass_kernel_spmd

    x, W, tok_b, g, b, w_qkv, w_out, b_out, rk, Wg, bg, W1, b1, W2, b2 = (np.asarray(i) for i in (
        x, L0_tok_W, L0_tok_b, L0_attn_ln_g, L0_attn_ln_b, L0_attn_w_qkv, L0_attn_w_out, L0_attn_b_out,
        L0_attn_res_kernel, L0_ffn_Wg, L0_ffn_bg, L0_ffn_W1, L0_ffn_b1, L0_ffn_W2, L0_ffn_b2))
    patches = x.reshape(IMAGES, 3, 4, 16, 4, 16).transpose(1, 3, 5, 0, 2, 4).reshape(CHUNKS, 128, IMAGES, TOKENS)
    rows = np.zeros((CHUNKS, 128, IMAGES, ROWS), np.float32)
    rows[..., 1:] = patches
    rows = rows.reshape(CHUNKS, 128, ALL_ROWS).transpose(1, 0, 2)
    x_l = np.concatenate([rows[:, :, OFF[t]:OFF[t] + R[t]].reshape(128, -1) for t in range(TILES)], axis=1)

    wout_bd = np.zeros((2, 4, DH, 4, D), np.float32)
    for j in range(4):
        wout_bd[:, j, :, j, :] = w_out.reshape(2, 4, DH, D)[:, j]
    toep = np.zeros((PER_TILE, ROWS, HEADS, ROWS), np.float32)
    for j in range(TOKENS):
        for i in range(TOKENS):
            toep[:, 1 + j, :, 1 + i] = rk[:, 0, j - i + 16, 0]
    p128 = pack(128, P128, dict(
        tokw=W.T.reshape(CHUNKS, 128, D).transpose(1, 0, 2).reshape(128, -1),
        wvT=w_qkv[:, 2 * HEADS * DH:].T.reshape(2, 128, D).transpose(1, 0, 2).reshape(128, -1),
        woutbd=wout_bd.reshape(2, 128, 4 * D).transpose(1, 0, 2).reshape(128, -1),
        w2=W2.transpose(1, 0, 2).reshape(HIDDEN, -1)))
    p65 = pack(D + 1, P65, dict(
        wqk=w_qkv[:, :2 * HEADS * DH],
        ln=np.stack([g, b], axis=1),
        wg=np.concatenate([Wg, bg[None, :]], axis=0),
        w1=np.concatenate([W1.transpose(1, 0, 2).reshape(D, -1), b1.reshape(1, -1)], axis=0)))
    p119 = pack(RMAX, P119, dict(
        tokb=np.broadcast_to(tok_b, (RMAX, D)), bout=np.broadcast_to(b_out, (RMAX, D)),
        toep=toep.reshape(RMAX, -1)))

    arrays = {"x_l": x_l, "p128": p128, "p65": p65, "p119": p119, "b2": np.ascontiguousarray(b2),
              "cst": shape_constants()}
    nc = bacc.Bacc("TRN2", target_bir_lowering=False, num_devices=1)
    args = [nc.dram_tensor(f"{n}_dram", a.shape, F32, kind="ExternalInput").ap() for n, a in arrays.items()]
    out = nc.dram_tensor("out_dram", [ALL_ROWS, D], F32, kind="ExternalOutput").ap()
    vit_layer(nc, *args, out)
    r = run_bass_kernel_spmd(nc, [{f"{n}_dram": a for n, a in arrays.items()}], core_ids=[0])
    got = r.results[0]["out_dram"]
    return np.ascontiguousarray(got.reshape(IMAGES, ROWS, D)[:, 1:, :])
```

```python
from contextlib import ExitStack

import numpy as np

import concourse.bass as bass
from concourse import mybir

F32 = mybir.dt.float32
BF16 = mybir.dt.bfloat16
F16 = mybir.dt.float16
ALU = mybir.AluOpType
ACT = mybir.ActivationFunctionType
AX = mybir.AxisListType.X

IMAGES = 32
TOKENS = 16
PADS = 112
ROWS = TOKENS + 1
PER_TILE = 7
TILES = -(-IMAGES // PER_TILE)
D = 64
HEADS = 8
DH = 32
CHUNKS = 6
EXPERTS = 8
HIDDEN = 128
ITERS = 6
EPS = 1e-5
BLOCKS = [min(PER_TILE, IMAGES - PER_TILE * t) for t in range(TILES)]
R = [ROWS * n for n in BLOCKS]
OFF = [ROWS * PER_TILE * t for t in range(TILES)]
RMAX = R[0]
ALL_ROWS = ROWS * IMAGES
C = HEADS * ROWS
WIDE = 128
ALPHA = 3.5
FAR = float(2.0 ** 100)

P128 = dict(tokw=CHUNKS * D, wvT=2 * D, woutbd=2 * 4 * D, w2=EXPERTS * D)
P65 = dict(wqk=2 * HEADS * DH, ln=2, wg=EXPERTS, w1=EXPERTS * HIDDEN)
P119 = dict(tokb=D, bout=D, toep=C)
CST = dict(ident=128, blocks=RMAX, wcol=ROWS, wsym=ROWS, eye=ROWS, selw=PER_TILE, winv=ROWS,
           before=EXPERTS * EXPERTS, farl=RMAX, farr=RMAX)


def starts(widths):
    out, at = {}, 0
    for name, w in widths.items():
        out[name] = (at, at + w)
        at += w
    return out, at


def vit_layer(nc, x_in, p128_in, p65_in, p119_in, b2_in, cst_in, out):
    with ExitStack() as ctx:
        def sb(name, shape, dt=F32):
            return ctx.enter_context(nc.sbuf_tensor(name, shape, dt))

        def sem(name):
            return ctx.enter_context(nc.semaphore(name))

        x_sb = sb("x_sb", [128, CHUNKS * ALL_ROWS])
        col128, n128 = starts(P128)
        col65, n65 = starts(P65)
        col119, n119 = starts(P119)
        colc, nc_ = starts(CST)
        p128 = sb("p128", [128, n128])
        p65 = sb("p65", [128, n65])
        p119 = sb("p119", [RMAX, n119])
        b2 = sb("b2", [128, D])
        cst = sb("cst", [128, nc_])

        def v128(name):
            return p128[:, col128[name][0]:col128[name][1]]

        def v65(name, rows=D):
            return p65[0:rows, col65[name][0]:col65[name][1]]

        def v119(name):
            return p119[:, col119[name][0]:col119[name][1]]

        def const(name, rows=128):
            return cst[0:rows, colc[name][0]:colc[name][1]]

        tokw = v128("tokw").rearrange("p (c e) -> p c e", c=CHUNKS)
        wvT = v128("wvT").rearrange("p (c e) -> p c e", c=2)
        woutbd = v128("woutbd").rearrange("p (c n) -> p c n", c=2)
        w2 = v128("w2").rearrange("p (e d) -> p e d", e=EXPERTS)
        wqk = v65("wqk", 128).rearrange("p (c m) -> p c m", c=4)
        wg = v65("wg", 128)
        w1 = v65("w1", 128).rearrange("p (e h) -> p e h", e=EXPERTS)
        toep = v119("toep").rearrange("p (h c) -> p h c", h=HEADS)
        ident = const("ident")

        h = sb("h", [RMAX, TILES, D])
        base = sb("base", [RMAX, TILES, D])
        h2 = sb("h2", [RMAX, TILES, D])
        conv = sb("conv", [RMAX, TILES, D])
        att = sb("att", [RMAX, D])
        resT = sb("resT", [D, ALL_ROWS])
        stats = sb("stats", [RMAX, TILES, 6])
        moments = sb("moments", [RMAX, TILES, 2])
        powarg = sb("powarg", [RMAX, TILES, 2])
        rstd = sb("rstd", [RMAX, TILES, 2])
        exponent = sb("exponent", [RMAX, 2])
        warm = sb("warm", [RMAX, 2])
        xc = sb("xc", [RMAX, TILES, D])
        xnT = sb("xnT", [128, ALL_ROWS])
        qT = sb("qT", [128, 2, 2, RMAX])
        kT = sb("kT", [128, 2, 2, 4, RMAX])
        wvo = sb("wvo", [128, HEADS * D])
        v = sb("v", [RMAX, TILES, HEADS * D])
        score = sb("score", [RMAX, 2, HEADS, ROWS])
        smax = sb("smax", [RMAX, 2, HEADS])
        e = sb("e", [RMAX, 2, HEADS, ROWS])
        z = sb("z", [RMAX, 2, HEADS])
        rz = sb("rz", [RMAX, 2, HEADS])
        a = sb("a", [RMAX, TILES, HEADS, ROWS])
        peaks = sb("peaks", [RMAX, 2, TILES])
        colw = sb("colw", [PER_TILE, TILES, HEADS, ROWS])
        peak = sb("peak", [RMAX, 2])
        peak2 = sb("peak2", [2, 1])
        peakd = sb("peakd", [2, 2])
        scale = sb("scale", [RMAX, 1])
        rscale = sb("rscale", [RMAX, 1])
        ones2 = sb("ones2", [2, RMAX])
        bd = sb("bd", [RMAX, TILES, 2, HEADS, WIDE], F16)
        bd2 = sb("bd2", [RMAX, TILES, 2, HEADS, WIDE], F16)
        aT = sb("aT", [RMAX, TILES, 2, HEADS, WIDE], F16)
        a16 = sb("a16", [RMAX, TILES, 2, HEADS, ROWS], F16)
        x16 = sb("x16", [RMAX, TILES, 2, HEADS, ROWS], F16)
        x2_16 = sb("x2_16", [RMAX, TILES, 2, HEADS, ROWS], F16)
        w16 = sb("w16", [RMAX, TILES, 2, HEADS, ROWS], F16)
        eye16 = sb("eye16", [RMAX, ROWS], F16)
        blocks16 = sb("blocks16", [RMAX, RMAX], F16)
        ident16 = sb("ident16", [128, 128], F16)
        v3 = sb("v3", [RMAX, TILES, 3, HEADS * D], BF16)
        vrest = sb("vrest", [RMAX, 2, HEADS * D])
        toepbd = sb("toepbd", [RMAX, HEADS, RMAX])
        xm = sb("xm", [RMAX, TILES, HEADS, ROWS])
        xw = sb("xw", [RMAX, TILES, HEADS, ROWS])
        yv3 = sb("yv3", [RMAX, 2, 3, HEADS * D], BF16)
        yvrest = sb("yvrest", [RMAX, 2, HEADS * D])
        farl = sb("farl", [128, RMAX], BF16)
        farr = sb("farr", [128, 4, RMAX], BF16)
        zn = sb("zn", [RMAX, TILES, D])
        zT = sb("zT", [128, TILES, RMAX])
        gate = sb("gate", [RMAX, EXPERTS])
        ahead = sb("ahead", [RMAX, 2, EXPERTS, EXPERTS])
        rank = sb("rank", [RMAX, EXPERTS])
        pick = sb("pick", [RMAX, TILES, EXPERTS])
        pickT = sb("pickT", [128, 2, RMAX])
        pickTb = sb("pickTb", [128, 2, RMAX], BF16)
        onehot = sb("onehot", [128, EXPERTS, HIDDEN], BF16)
        hid = sb("hid", [HIDDEN, 2, EXPERTS, RMAX])
        hidm = sb("hidm", [HIDDEN, 2, EXPERTS, RMAX])

        ps = ctx.enter_context(nc.psum_tensor("ps", [128, 8, 512], F32))

        def bank(b, rows, cols):
            return ps[0:rows, b, 0:cols]

        B_EMB, B_XT, B_QK, B_V = 0, 1, 1, 2
        B_SCORE = 3
        B_GRAM = 5
        B_AT = 6
        B_WVO, B_PEAK, B_TOEP = 3, 0, 1
        def B_ITER(t): return 2 + t
        def B_YV(t): return t % 2
        B_ATT, B_FFN, B_MISC, B_UP, B_PICK = 2, 2, 3, 4, 6
        AT_FFN = 3 * D

        x_in_sem = [sem(f"x_loaded{t}") for t in range(TILES)]
        tokw_loaded, wv_loaded, p65_loaded = sem("tokw_loaded"), sem("wv_loaded"), sem("p65_loaded")
        p119_loaded, cst_loaded, ffn_loaded = sem("p119_loaded"), sem("cst_loaded"), sem("ffn_loaded")
        bias_loaded, tokb_loaded = sem("bias_loaded"), sem("tokb_loaded")
        stored = sem("stored")
        wvo_done, emb_done, xt_done, qk_done, v_done = (sem(n) for n in (
            "wvo_done", "emb_done", "xt_done", "qk_done", "v_done"))
        score_done, gram_done, at_done = sem("score_done"), sem("gram_done"), sem("at_done")
        toep_done, peakT_done, peakb_done = sem("toep_done"), sem("peakT_done"), sem("peakb_done")
        x2_done, prod_done = sem("x2_done"), sem("prod_done")
        yv_done, att_done, zt_done, gate_done = (sem(n) for n in ("yv_done", "att_done", "zt_done", "gate_done"))
        up_done, pickT_done, pickb_done, ffn_done = (sem(n) for n in (
            "up_done", "pickT_done", "pickb_done", "ffn_done"))
        dve_step = sem("dve_step")
        conv_read, base_complete = sem("conv_read"), sem("base_complete")
        setup_done, choose_step = sem("setup_done"), sem("choose_step")
        emb_read, arg_ready, xc_ready = sem("emb_read"), sem("arg_ready"), sem("xc_ready")
        k_ready, score_ready, score_read = sem("k_ready"), sem("score_ready"), sem("score_read")
        a_ready, abd_ready = sem("a_ready"), sem("abd_ready")
        peak_ready, peakd_ready = sem("peak_ready"), sem("peakd_ready")
        ah_ready = sem("ah_ready")
        al_ready = sem("al_ready")
        x_ready, xbd_ready, w_ready, x2l_ready, x2bd_ready = (sem(n) for n in (
            "x_ready", "xbd_ready", "w_ready", "x2l_ready", "x2bd_ready"))
        xh_ready, x2h_ready, wh_ready = sem("xh_ready"), sem("x2h_ready"), sem("wh_ready")
        xl_ready, wl_ready = sem("xl_ready"), sem("wl_ready")
        x2bd_act_ready = sem("x2bd_act_ready")
        v_cut, v_cut_step = sem("v_cut"), sem("v_cut_step")
        yv1_ready, yvrest_ready, yv2_ready, yv3_ready = (sem(n) for n in (
            "yv1_ready", "yvrest_ready", "yv2_ready", "yv3_ready"))
        h2_read, arg2_ready, zn_ready = sem("h2_read"), sem("arg2_ready"), sem("zn_ready")
        gate_read, pick_ready, pickT_ready, hidm_ready, res_ready = (sem(n) for n in (
            "gate_read", "pick_ready", "pickT_ready", "hidm_ready", "res_ready"))
        wvo_ready, xnT_ready, qk_ready, v_ready, e_ready = (sem(n) for n in (
            "wvo_ready", "xnT_ready", "qk_ready", "v_ready", "e_ready"))
        cols_ready, gram_read, at_ready = sem("cols_ready"), sem("gram_read"), sem("at_ready")
        zT_ready, hid_ready = sem("zT_ready"), sem("hid_ready")
        xbd_act_ready = sem("xbd_act_ready")
        pool_setup, rstd_ready, rstd2_ready, base_ready, base_step = (sem(n) for n in (
            "pool_setup", "rstd_ready", "rstd2_ready", "base_ready", "base_step"))

        def x_tile(t, c):
            at = CHUNKS * OFF[t] + c * R[t]
            return x_sb[:, at:at + R[t]]

        def blocks(t, ap):
            return ap[:, :, None, :].broadcast_to([R[t], ap.shape[1], BLOCKS[t], ROWS])

        def mask(t, heads=HEADS):
            m = const("blocks", R[t])[:, 0:R[t]].rearrange("p (g c) -> p g c", c=ROWS)
            return m[:, None, :, :].broadcast_to([R[t], heads, BLOCKS[t], ROWS])

        def spread(engine_tt, dst, src, t, n):
            r = slice(0, R[t])
            shape = [R[t], 2 * HEADS, n, ROWS]
            m = blocks16[r, 0:n * ROWS].rearrange("p (g c) -> p g c", c=ROWS)
            return engine_tt(
                dst[r, t, :, :, 0:n * ROWS].rearrange("p s h (g c) -> p (s h) g c", c=ROWS),
                src[r, t].rearrange("p s h c -> p (s h) c")[:, :, None, :].broadcast_to(shape),
                m[:, None, :, :].broadcast_to(shape), ALU.mult)

        def by_image(ap):
            return ap.rearrange("p h (g c) -> p h g c", c=ROWS)

        ACT_BLOCKS = 2
        block = ctx.enter_context(nc.Block())

        fills = [("exponent", exponent[:], -0.5), ("xnT", xnT[:], 0.0), ("p65", p65[D:, :], 0.0),
                 ("wvo", wvo[D:, :], 0.0), ("kT", kT[:], 0.0),
                 ("peaks", peaks[:], 0.0), ("ones2", ones2[:], 1.0),
                 ("b2", b2[:], 0.0), ("pickT", pickT[:], 0.0),
                 ("pickTb", pickTb[:], 0.0),
                 ("bd", bd[:, 0:TILES - 1, :, :, RMAX:], 0.0), ("bd", bd[:, TILES - 1, :, :, R[-1]:], 0.0),
                 ("aT", aT[:, 0:TILES - 1, :, :, RMAX:], 0.0), ("aT", aT[:, TILES - 1, :, :, R[-1]:], 0.0),
                 ("v", v[64:RMAX, TILES - 1, :], 0.0), ("base", base[64:RMAX, TILES - 1, :], 0.0),
                 ("bd2", bd2[:, 0:TILES - 1, :, :, RMAX:], 0.0), ("bd2", bd2[:, TILES - 1, :, :, R[-1]:], 0.0),
                 ("zT", zT[D:, :, :], 0.0), ("zT", zT[D:D + 1, :, :], 1.0)]

        def filled(name):
            return max(n + 1 for n, fill in enumerate(fills) if fill[0] == name)

        @block.sync
        def _(sp):
            sp.dma_start(p128[:, 0:CHUNKS * D], p128_in[:, 0:CHUNKS * D]).then_inc(tokw_loaded, 16)
            for t in range(TILES):
                cols = slice(CHUNKS * OFF[t], CHUNKS * (OFF[t] + R[t]))
                sp.dma_start(x_sb[:, cols], x_in[:, cols]).then_inc(x_in_sem[t], 16)
            sp.wait_ge(pool_setup, filled("p65"))
            bias_row = slice(col65["wg"][0], n65)
            sp.dma_start(p65[D:D + 1, bias_row], p65_in[D:D + 1, bias_row]).then_inc(bias_loaded, 16)
            sp.wait_ge(pool_setup, filled("b2"))
            sp.dma_start(b2[0:EXPERTS, :], b2_in).then_inc(bias_loaded, 16)
            for t in range(TILES):
                sp.wait_ge(res_ready, t + 1)
                cols = slice(OFF[t], OFF[t] + R[t])
                sp.dma_start(out[:, cols], resT[:, cols]).then_inc(stored, 16)
            sp.wait_ge(stored, 16 * TILES)

        @block.gpsimd
        def _(pool):
            def fill(n):
                if n:
                    pool.wait_ge(pool_setup, n)
                nc.gpsimd.memset(fills[n][1], fills[n][2]).then_inc(pool_setup, 1)

            def rstd_of(t):
                r = slice(0, R[t])
                pool.wait_ge(arg_ready, 2 * (t + 1))
                nc.gpsimd.tensor_tensor(rstd[r, t, :], powarg[r, t, :], exponent[r, :],
                                        ALU.pow).then_inc(rstd_ready, 1)

            first = filled("kT")
            for n in range(first):
                fill(n)

            def base_of(t):
                r = slice(0, R[t])
                if t == 0:
                    pool.wait_ge(p119_loaded, 16)
                pool.wait_ge(xc_ready, 2 * (t + 1))
                nc.gpsimd.tensor_tensor(base[r, t, :], h[r, t, :], v119("bout")[r, :],
                                        ALU.add).then_inc(base_step, 1)
                pool.wait_ge(base_step, t + 1)
                nc.gpsimd.tensor_tensor(base[r, t, :], base[r, t, :], h2[r, t, :],
                                        ALU.add).then_inc(base_ready, 1)

            def cut_v(t):
                r = slice(0, R[t])
                pool.wait_ge(v_ready, t + 1)
                nc.gpsimd.tensor_copy(v3[r, t, 0], v[r, t]).then_inc(v_cut_step, 1)
                pool.wait_ge(v_cut_step, 3 * t + 1)
                nc.gpsimd.tensor_tensor(vrest[r, t % 2], v[r, t], v3[r, t, 0], ALU.subtract).then_inc(v_cut_step, 1)
                pool.wait_ge(v_cut_step, 3 * t + 2)
                nc.gpsimd.tensor_copy(v3[r, t, 1], vrest[r, t % 2]).then_inc(v_cut_step, 1)
                pool.wait_ge(v_cut_step, 3 * t + 3)
                nc.gpsimd.tensor_tensor(v3[r, t, 2], vrest[r, t % 2], v3[r, t, 1], ALU.subtract).then_inc(v_cut, 1)

            pool.wait_ge(pool_setup, first)
            rstd_of(0)
            for s in range(TILES + 1):
                if s + 1 < TILES:
                    rstd_of(s + 1)
                if s == 0:
                    for n in range(first, len(fills)):
                        fill(n)
                    pool.wait_ge(pool_setup, len(fills))
                if s >= 1:
                    cut_v(s - 1)
            for t in range(TILES):
                base_of(t)

            def second_x(t, count):
                pool.wait_ge(xh_ready, count)
                nc.gpsimd.tensor_tensor(x16[0:R[t], t, 1], xm[0:R[t], t], x16[0:R[t], t, 0], ALU.subtract
                                        ).then_inc(xl_ready, 1)

            for t in range(TILES):
                second_x(t, t + 1)
            with pool.Fori(0, ITERS) as it:
                for t in range(TILES):
                    pool.wait_ge(wh_ready, it * TILES + (t + 1))
                    nc.gpsimd.tensor_tensor(w16[0:R[t], t, 1], xw[0:R[t], t], w16[0:R[t], t, 0], ALU.subtract
                                            ).then_inc(wl_ready, 1)
                for t in range(TILES):
                    second_x(t, it * TILES + (TILES + t + 1))
            pool.wait_ge(conv_read, 1)
            pool.wait_ge(base_ready, TILES)
            nc.gpsimd.tensor_tensor(base[:, :, :], base[:, :, :], conv[:, :, :], ALU.add).then_inc(base_complete, 1)

            def third_yv(t):
                r, p = slice(0, R[t]), t % 2
                pool.wait_ge(yv2_ready, t + 1)
                nc.gpsimd.tensor_tensor(yv3[r, p, 2], yvrest[r, p], yv3[r, p, 1], ALU.subtract
                                        ).then_inc(yv3_ready, 1)

            third_yv(0)
            third_yv(1)
            for t in range(TILES):
                r = slice(0, R[t])
                pool.wait_ge(arg2_ready, t + 1)
                nc.gpsimd.tensor_tensor(rstd[r, t, 0:1], powarg[r, t, 0:1], exponent[r, 0:1],
                                        ALU.pow).then_inc(rstd2_ready, 1)
                if t + 2 < TILES:
                    third_yv(t + 2)

        @block.scalar
        def _(act):
            act.dma_start(p119[:, 0:D], p119_in[:, 0:D]).then_inc(tokb_loaded, 16)
            act.dma_start(cst[:, :], cst_in).then_inc(cst_loaded, 16)
            early, late = slice(0, col65["w1"][0]), slice(col65["w1"][0], n65)
            act.dma_start(p65[0:D, early], p65_in[0:D, early]).then_inc(p65_loaded, 16)
            wv = slice(col128["wvT"][0], col128["w2"][0])
            act.dma_start(p128[:, wv], p128_in[:, wv]).then_inc(wv_loaded, 16)
            act.dma_start(p119[:, D:], p119_in[:, D:]).then_inc(p119_loaded, 16)
            act.dma_start(p65[0:D, late], p65_in[0:D, late]).then_inc(ffn_loaded, 16)
            act.dma_start(p128[:, col128["w2"][0]:], p128_in[:, col128["w2"][0]:]).then_inc(ffn_loaded, 16)
            ln = v65("ln")
            act.wait_ge(pool_setup, filled("exponent"))
            nc.scalar.activation(warm[:, :], exponent[:, :], ACT.Exp)

            def turned(t):
                if t == 0:
                    act.wait_ge(p65_loaded, 16)
                    act.wait_ge(pool_setup, filled("xnT"))
                act.wait_ge(xt_done, t + 1)
                cols = slice(OFF[t], OFF[t] + R[t])
                nc.scalar.activation(
                    xnT[0:D, cols].rearrange("p (n s) -> p n s", s=ROWS)[:, :, 1:ROWS],
                    bank(B_XT, D, R[t]).rearrange("p (n s) -> p n s", s=ROWS)[:, :, 1:ROWS],
                    ACT.Identity, bias=ln[:, 1:2], scale=ln[:, 0:1]).then_inc(xnT_ready, 1)

            def q_k_out(t):
                p = t % 2
                if t == 0:
                    act.wait_ge(pool_setup, filled("kT"))
                    act.wait_ge(wvo_done, 1)
                    nc.scalar.copy(wvo[0:D, :], bank(B_WVO, D, HEADS * D)).then_inc(wvo_ready, 1)
                act.wait_ge(qk_done, t + 1)
                if t >= 2:
                    act.wait_ge(score_done, 2 * (t - 1))
                nc.scalar.activation(qT[:, p, :, 0:R[t]],
                                     bank(B_QK, 128, 2 * R[t]).rearrange("p (c n) -> p c n", c=2),
                                     ACT.Copy, scale=DH ** -0.5).then_inc(qk_ready, 1)
                for j in range(4):
                    rows = slice(DH * j, DH * j + DH)
                    nc.scalar.copy(kT[rows, p, :, j, 0:R[t]],
                                   ps[rows, B_QK, 2 * R[t]:4 * R[t]].rearrange("p (c n) -> p c n", c=2)
                                   ).then_inc(qk_ready, 1)

            def v_out(t):
                r = slice(0, R[t])
                act.wait_ge(v_done, t + 1)
                nc.scalar.copy(v[r, t, :], bank(B_V, R[t], HEADS * D)).then_inc(v_ready, 1)

            def softmax_exp(t):
                act.wait_ge(score_ready, t + 1)
                nc.scalar.activation(e[0:R[t], t % 2], score[0:R[t], t % 2], ACT.Exp).then_inc(e_ready, 1)

            def first_a(t):
                act.wait_ge(a_ready, 2 * t + 1)
                nc.scalar.copy(a16[0:R[t], t, 0], a[0:R[t], t]).then_inc(ah_ready, 1)

            def gram_out(t):
                act.wait_ge(gram_done, t + 1)
                nc.scalar.copy(colw[0:BLOCKS[t], t], bank(B_GRAM, BLOCKS[t], C).rearrange(
                    "p (h c) -> p h c", c=ROWS)).then_inc(cols_ready, 1)
                nc.scalar.copy(xm[0:R[t], t], ps[0:R[t], B_GRAM, C:2 * C].rearrange(
                    "p (h c) -> p h c", c=ROWS)).then_inc(gram_read, 1)

            def turned_a(t, part):
                if t == 0 and part == 0:
                    act.wait_ge(pool_setup, filled("aT"))
                act.wait_ge(at_done, 2 * t + part + 1)
                nc.scalar.copy(aT[0:R[t], t, part, :, 0:R[t]],
                               ps[0:R[t], B_AT + part, :].bitcast(F16).rearrange("p (h n) -> p h n", h=HEADS)[:, :, 0:R[t]]
                               ).then_inc(at_ready, 1)

            for s in range(TILES + 2):
                if s < TILES:
                    turned(s)
                if s >= 2:
                    gram_out(s - 2)
                if 1 <= s <= TILES:
                    softmax_exp(s - 1)
                if s >= 2:
                    turned_a(s - 2, 0)
                if s < TILES:
                    q_k_out(s)
                if 1 <= s <= TILES:
                    first_a(s - 1)
                if s >= 2:
                    turned_a(s - 2, 1)
                if s < TILES:
                    v_out(s)

            act.wait_ge(toep_done, 1)
            nc.scalar.copy(conv[:, :, :], bank(B_TOEP, RMAX, TILES * D).rearrange("p (t d) -> p t d", t=TILES)
                           ).then_inc(conv_read, 1)

            def spread_last(dst, src, t):
                r = slice(0, R[t])
                for g in range(BLOCKS[t] - ACT_BLOCKS, BLOCKS[t]):
                    last = nc.scalar.activation(
                        dst[r, t, :, :, ROWS * g:ROWS * g + ROWS].rearrange("p s h c -> p (s h) c"),
                        src[r, t].rearrange("p s h c -> p (s h) c"), ACT.Copy,
                        scale=const("blocks", R[t])[:, ROWS * g:ROWS * g + 1])
                return last

            def first_x(t, count):
                act.wait_ge(x_ready, count)
                nc.scalar.copy(x16[0:R[t], t, 0], xm[0:R[t], t]).then_inc(xh_ready, 1)

            def spread_x(t, count):
                act.wait_ge(xl_ready, count)
                spread_last(bd, x16, t).then_inc(xbd_act_ready, 1)

            def first_x2_w(t, count):
                r = slice(0, R[t])
                act.wait_ge(w_ready, count)
                nc.scalar.activation(x2_16[r, t, 0], ps[r, B_ITER(t), 0:C].rearrange("p (h c) -> p h c", c=ROWS),
                                     ACT.Copy, scale=-1.0 / 7.0).then_inc(x2h_ready, 1)
                nc.scalar.copy(w16[r, t, 0], xw[r, t]).then_inc(wh_ready, 1)

            def spread_x2(t, count):
                act.wait_ge(x2l_ready, count)
                spread_last(bd2, x2_16, t).then_inc(x2bd_act_ready, 1)

            for t in range(TILES):
                first_x(t, t + 1)
                if t >= 1:
                    spread_x(t - 1, t)
            with act.Fori(0, ITERS) as it:
                for t in range(TILES):
                    first_x2_w(t, it * TILES + (t + 1))
                    if t == 0:
                        spread_x(TILES - 1, it * TILES + TILES)
                    else:
                        spread_x2(t - 1, it * TILES + t)
                for t in range(TILES):
                    first_x(t, it * TILES + (TILES + t + 1))
                    if t == 0:
                        spread_x2(TILES - 1, it * TILES + TILES)
                    else:
                        spread_x(t - 1, it * TILES + (TILES + t))
            spread_x(TILES - 1, (ITERS + 1) * TILES)

            def first_yv(t):
                act.wait_ge(yv_done, t + 1)
                if t >= 2:
                    act.wait_ge(att_done, t - 1)
                nc.scalar.activation(yv3[0:R[t], t % 2, 0], bank(B_YV(t), R[t], HEADS * D), ACT.Copy,
                                     scale=1.0 / ALPHA).then_inc(yv1_ready, 1)

            def second_yv(t):
                act.wait_ge(yvrest_ready, t + 1)
                nc.scalar.copy(yv3[0:R[t], t % 2, 1], yvrest[0:R[t], t % 2]).then_inc(yv2_ready, 1)

            def gelu(t, half):
                act.wait_ge(up_done, 2 * t + half + 1)
                if t >= 2 and half == 0:
                    act.wait_ge(hidm_ready, 2 * (t - 1))
                nc.scalar.activation(hid[:, t % 2, 4 * half:4 * half + 4, 0:R[t]],
                                     bank(B_UP + half, HIDDEN, 4 * R[t]).rearrange("p (e n) -> p e n", e=4),
                                     ACT.Gelu).then_inc(hid_ready, 1)

            def pick_out(t):
                p = t % 2
                act.wait_ge(pickT_done, t + 1)
                if t >= 2:
                    act.wait_ge(ffn_done, t - 1)
                src = bank(B_MISC, EXPERTS, R[t])
                nc.scalar.copy(pickTb[0:EXPERTS, p, 0:R[t]], src).then_inc(pickT_ready, 1)
                nc.scalar.copy(pickT[0:EXPERTS, p, 0:R[t]], src).then_inc(pickT_ready, 1)

            def z_out(t):
                act.wait_ge(zt_done, t + 1)
                nc.scalar.copy(zT[0:D, t, 0:R[t]], bank(B_MISC, D, R[t])).then_inc(zT_ready, 1)

            def result(t):
                act.wait_ge(ffn_done, t + 1)
                nc.scalar.copy(resT[:, OFF[t]:OFF[t] + R[t]], ps[0:D, B_FFN, AT_FFN:AT_FFN + R[t]]).then_inc(res_ready, 1)

            for t in range(2):
                first_yv(t)
                second_yv(t)
            nc.scalar.activation(warm[:, :], exponent[:, :], ACT.Gelu)
            for s in range(1, TILES + 2):
                if s >= 2:
                    gelu(s - 2, 0)
                    pick_out(s - 2)
                    gelu(s - 2, 1)
                if s + 1 < TILES:
                    first_yv(s + 1)
                if s <= TILES:
                    z_out(s - 1)
                if s + 1 < TILES:
                    second_yv(s + 1)
                if s >= 2:
                    result(s - 2)

        @block.vector
        def _(dve):
            steps = [0]

            def own(instruction):
                steps[0] += 1
                instruction.then_inc(dve_step, 1)
                dve.wait_ge(dve_step, steps[0])

            tt, ts, stt = nc.vector.tensor_tensor, nc.vector.tensor_scalar, nc.vector.scalar_tensor_tensor
            def layernorm_stats(t, src):
                r = slice(0, R[t])
                own(nc.vector.bn_stats(stats[r, t, :], src))
                own(nc.vector.bn_aggr(moments[r, t, :], stats[r, t, :]))

            def masks():
                dve.wait_ge(cst_loaded, 16)
                nc.vector.tensor_copy(farl[:, :], const("farl")).then_inc(setup_done, 1)
                nc.vector.tensor_copy(farr[:, :, :], const("farr")[:, None, :].broadcast_to([128, 4, RMAX])
                                      ).then_inc(setup_done, 1)
                nc.vector.tensor_copy(blocks16[:, :], const("blocks", RMAX)).then_inc(setup_done, 1)
                nc.vector.tensor_copy(ident16[:, :], ident).then_inc(setup_done, 1)

            def other_constants():
                nc.vector.tensor_copy(onehot[:, :, :],
                                      ident[:, 0:EXPERTS][:, :, None].broadcast_to([128, EXPERTS, HIDDEN])).then_inc(setup_done, 1)
                nc.vector.tensor_copy(eye16[:, :], const("eye", RMAX)).then_inc(setup_done, 1)
                dve.wait_ge(p119_loaded, 16)
                tt(by_image(toepbd[:, :, :]), blocks(0, toep), mask(0), ALU.mult).then_inc(setup_done, 1)

            def embed(t):
                r = slice(0, R[t])
                if t == 0:
                    dve.wait_ge(tokb_loaded, 16)
                dve.wait_ge(emb_done, t + 1)
                tt(h[r, t, :], bank(B_EMB, R[t], D), v119("tokb")[r, :], ALU.add).then_inc(emb_read, 1)
                dve.wait_ge(emb_read, t + 1)
                layernorm_stats(t, h[r, t, :])
                ts(powarg[r, t, 0:1], moments[r, t, 1:2], EPS, None, ALU.add).then_inc(arg_ready, 1)
                ts(powarg[r, t, 1:2], moments[r, t, 1:2], 1.0 + EPS, EPS * EPS, ALU.mult, ALU.add
                   ).then_inc(arg_ready, 1)

            def normalise(t):
                r = slice(0, R[t])
                dve.wait_ge(rstd_ready, t + 1)
                ts(xc[r, t, :], h[r, t, :], moments[r, t, 0:1], rstd[r, t, 1:2], ALU.subtract, ALU.mult
                   ).then_inc(xc_ready, 1)
                ts(h2[r, t, :], h[r, t, :], moments[r, t, 0:1], rstd[r, t, 0:1], ALU.subtract, ALU.mult
                   ).then_inc(xc_ready, 1)

            def scores_out(t):
                r = slice(0, R[t])
                p = t % 2
                if t >= 2:
                    dve.wait_ge(e_ready, t - 1)
                for c in range(2):
                    dve.wait_ge(score_done, 2 * t + c + 1)
                    nc.vector.tensor_reduce(
                        score[r, p, 4 * c:4 * c + 4, :],
                        bank(B_SCORE + c, R[t], 4 * R[t]).rearrange("p (h g c) -> p h c g", h=4, c=ROWS),
                        AX, ALU.max).then_inc(score_read, 1)
                dve.wait_ge(score_read, 2 * (t + 1))
                own(nc.vector.tensor_reduce(smax[r, p, :], score[r, p], AX, ALU.max))
                tt(score[r, p], score[r, p], smax[r, p, :, None].broadcast_to([R[t], HEADS, ROWS]),
                   ALU.subtract).then_inc(score_ready, 1)

            def softmax(t):
                r = slice(0, R[t])
                p = t % 2
                wcol = const("wcol", R[t])[:, None, :].broadcast_to([R[t], HEADS, ROWS])
                wsym = const("wsym", R[t])[:, None, :].broadcast_to([R[t], HEADS, ROWS])
                dve.wait_ge(e_ready, t + 1)
                own(tt(e[r, p], e[r, p], wcol, ALU.mult))
                own(nc.vector.tensor_reduce(z[r, p, :], e[r, p], AX, ALU.add))
                own(nc.vector.reciprocal(rz[r, p, :], z[r, p, :]))
                own(tt(e[r, p], e[r, p], rz[r, p, :, None].broadcast_to([R[t], HEADS, ROWS]), ALU.mult))
                tt(a[r, t], e[r, p], wsym, ALU.mult).then_inc(a_ready, 1)
                own(nc.vector.tensor_reduce(z[r, p, :], e[r, p], AX, ALU.add))
                nc.vector.tensor_reduce(peaks[r, 0, t:t + 1], z[r, p, :], AX, ALU.max).then_inc(a_ready, 1)

            def spread_a(t):
                r = slice(0, R[t])
                if t == 0:
                    dve.wait_ge(setup_done, 4)
                dve.wait_ge(ah_ready, t + 1)
                tt(a16[r, t, 1], a[r, t], a16[r, t, 0], ALU.subtract).then_inc(al_ready, 1)
                dve.wait_ge(al_ready, t + 1)
                spread(tt, bd, a16, t, BLOCKS[t]).then_inc(abd_ready, 1)

            embed(0)
            masks()
            normalise(0)
            for s in range(TILES + 2):
                if s >= 2:
                    spread_a(s - 2)
                if s + 1 < TILES:
                    embed(s + 1)
                if 1 <= s <= TILES:
                    scores_out(s - 1)
                if s + 1 < TILES:
                    normalise(s + 1)
                if s == 0:
                    other_constants()
                if 1 <= s <= TILES:
                    if s == 1:
                        dve.wait_ge(pool_setup, filled("peaks"))
                    softmax(s - 1)

            def column_peaks(tiles, rows):
                n = len(tiles)
                t0 = tiles[0]
                own(tt(colw[0:rows, t0:t0 + n].rearrange("p t h c -> p (t h) c"),
                       colw[0:rows, t0:t0 + n].rearrange("p t h c -> p (t h) c"),
                       const("winv", rows)[:, None, :].broadcast_to([rows, n * HEADS, ROWS]), ALU.mult))
                own(nc.vector.tensor_reduce(peaks[0:rows, 1, t0:t0 + n],
                                            colw[0:rows, t0:t0 + n].rearrange("p t h c -> p t (h c)"),
                                            AX, ALU.max))

            dve.wait_ge(cols_ready, TILES - 1)
            dve.wait_ge(a_ready, 2 * TILES)
            column_peaks(range(TILES - 1), PER_TILE)
            dve.wait_ge(cols_ready, TILES)
            column_peaks([TILES - 1], BLOCKS[-1])
            nc.vector.tensor_reduce(peak[:, :], peaks[:, :, :], AX, ALU.max).then_inc(peak_ready, 1)
            dve.wait_ge(peakT_done, 1)
            own(nc.vector.tensor_reduce(peak2[:, :], bank(B_PEAK, 2, RMAX), AX, ALU.max))
            ts(peakd[:, :], ident[0:2, 0:2], peak2[:, 0:1], None, ALU.mult).then_inc(peakd_ready, 1)
            dve.wait_ge(peakb_done, 1)
            own(nc.vector.tensor_reduce(scale[:, :], bank(B_PEAK, RMAX, 2), AX, ALU.mult))
            own(nc.vector.reciprocal(rscale[:, :], scale[:, :]))

            def new_x(t, count):
                r = slice(0, R[t])
                prod = ps[r, B_ITER(t), C:2 * C].rearrange("p (h c) -> p h c", c=ROWS)
                dve.wait_ge(prod_done, count)
                stt(xm[r, t], xm[r, t], 13.0 / 4.0, prod, ALU.mult, ALU.add).then_inc(x_ready, 1)

            def spread_x(t, count):
                dve.wait_ge(xl_ready, count)
                spread(tt, bd, x16, t, BLOCKS[t] - ACT_BLOCKS).then_inc(xbd_ready, 1)

            def new_w(t, count):
                r = slice(0, R[t])
                dve.wait_ge(x2_done, count)
                stt(xw[r, t], ps[r, B_ITER(t), 0:C].rearrange("p (h c) -> p h c", c=ROWS), 2.0 / 49.0, xm[r, t],
                    ALU.mult, ALU.subtract).then_inc(w_ready, 1)

            def second_x2(t, count):
                r = slice(0, R[t])
                dve.wait_ge(x2h_ready, count)
                stt(x2_16[r, t, 1], ps[r, B_ITER(t), 0:C].rearrange("p (h c) -> p h c", c=ROWS), -1.0 / 7.0,
                    x2_16[r, t, 0], ALU.mult, ALU.subtract).then_inc(x2l_ready, 1)

            def spread_x2(t, count):
                dve.wait_ge(x2l_ready, count)
                spread(tt, bd2, x2_16, t, BLOCKS[t] - ACT_BLOCKS).then_inc(x2bd_ready, 1)

            dve.wait_ge(gram_read, TILES)
            dve.wait_ge(at_done, 2 * TILES)
            for t in range(TILES):
                r = slice(0, R[t])
                ts(xm[r, t], xm[r, t], rscale[r, 0:1], ALPHA, ALU.mult, ALU.mult).then_inc(x_ready, 1)
                if t >= 1:
                    spread_x(t - 1, t)
            with dve.Fori(0, ITERS) as it:
                for t in range(TILES):
                    new_w(t, it * TILES + (t + 1))
                    if t == 0:
                        spread_x(TILES - 1, it * TILES + TILES)
                    else:
                        second_x2(t - 1, it * TILES + t)
                        spread_x2(t - 1, it * TILES + t)
                for t in range(TILES):
                    if t == 0:
                        second_x2(TILES - 1, it * TILES + TILES)
                    new_x(t, it * TILES + (t + 1))
                    if t == 0:
                        spread_x2(TILES - 1, it * TILES + TILES)
                    else:
                        spread_x(t - 1, it * TILES + (TILES + t))
            spread_x(TILES - 1, (ITERS + 1) * TILES)
            def rest_of_yv(t):
                r = slice(0, R[t])
                p = t % 2
                dve.wait_ge(yv1_ready, t + 1)
                if t >= 2:
                    dve.wait_ge(yv3_ready, t - 1)
                stt(yvrest[r, p], bank(B_YV(t), R[t], HEADS * D), 1.0 / ALPHA, yv3[r, p, 0], ALU.mult, ALU.subtract
                    ).then_inc(yvrest_ready, 1)

            def attention_out(t):
                r = slice(0, R[t])
                dve.wait_ge(att_done, t + 1)
                nc.vector.tensor_reduce(att[r], bank(B_ATT, R[t], 3 * D).rearrange("p (j d) -> p d j", j=3),
                                        AX, ALU.add).then_inc(h2_read, 1)
                dve.wait_ge(h2_read, t + 1)
                if t == 0:
                    dve.wait_ge(base_complete, 1)
                own(tt(h2[r, t, :], base[r, t, :], att[r], ALU.add))
                layernorm_stats(t, h2[r, t, :])
                ts(powarg[r, t, 0:1], moments[r, t, 1:2], EPS, None, ALU.add).then_inc(arg2_ready, 1)

            def normalise_h2(t):
                r = slice(0, R[t])
                dve.wait_ge(rstd2_ready, t + 1)
                ts(zn[r, t, :], h2[r, t, :], moments[r, t, 0:1], rstd[r, t, 0:1], ALU.subtract, ALU.mult
                   ).then_inc(zn_ready, 1)

            def choose(t):
                r = slice(0, R[t])
                shape = [R[t], EXPERTS, EXPERTS]
                dve.wait_ge(gate_done, t + 1)
                nc.vector.tensor_copy(gate[r, :], bank(B_MISC, R[t], EXPERTS)).then_inc(gate_read, 1)
                dve.wait_ge(gate_read, t + 1)
                other = gate[r, None, :].broadcast_to(shape)
                mine = gate[r, :, None].broadcast_to(shape)
                tied = ahead[r, 1]
                tt(ahead[r, 0], other, mine, ALU.is_gt).then_inc(choose_step, 1)
                own(tt(tied, other, mine, ALU.is_equal))
                own(tt(tied, tied, const("before", R[t]).rearrange("p (e j) -> p e j", e=EXPERTS), ALU.mult))
                dve.wait_ge(choose_step, t + 1)
                own(nc.vector.tensor_reduce(rank[r, :], ahead[r].rearrange("p k e j -> p e k j"),
                                            mybir.AxisListType.XY, ALU.add))
                ts(pick[r, t, :], rank[r, :], 2.0, None, ALU.is_lt).then_inc(pick_ready, 1)

            def pick_hidden(t, half):
                p = t % 2
                dve.wait_ge(pickb_done, 2 * t + half + 1)
                dve.wait_ge(hid_ready, 2 * t + half + 1)
                if t >= 2:
                    dve.wait_ge(ffn_done, t - 1)
                tt(hidm[:, p, 4 * half:4 * half + 4, 0:R[t]], hid[:, p, 4 * half:4 * half + 4, 0:R[t]],
                   bank(B_PICK + half, HIDDEN, 4 * R[t]).rearrange("p (e n) -> p e n", e=4), ALU.mult
                   ).then_inc(hidm_ready, 1)

            rest_of_yv(0)
            rest_of_yv(1)
            for s in range(1, TILES + 2):
                if s >= 2:
                    choose(s - 2)
                if s <= TILES:
                    attention_out(s - 1)
                    normalise_h2(s - 1)
                if s >= 2:
                    pick_hidden(s - 2, 0)
                    pick_hidden(s - 2, 1)
                if s + 1 < TILES:
                    rest_of_yv(s + 1)

        @block.tensor
        def _(pe):
            mm = nc.tensor.matmul

            def parts_product(out, stationary, moving, more=()):
                steps = [(stationary[:, i], moving[:, j]) for i in range(stationary.shape[1])
                         for j in range(moving.shape[1])] + list(more)
                for i, (lhsT, rhs) in enumerate(steps):
                    last = mm(out, lhsT, rhs, start=(i == 0), stop=(i == len(steps) - 1))
                return last

            def w_v_w_out():
                pe.wait_ge(wv_loaded, 16)
                for c in range(2):
                    last = mm(ps[0:D, B_WVO, c * 4 * D:(c + 1) * 4 * D], wvT[:, c, :], woutbd[:, c, :],
                              start=True, stop=True)
                last.then_inc(wvo_done, 1)

            def embed(t):
                pe.wait_ge(x_in_sem[t], 16)
                if t == 0:
                    pe.wait_ge(tokw_loaded, 16)
                if t >= 1:
                    pe.wait_ge(emb_read, t)
                for c in range(CHUNKS):
                    last = mm(bank(B_EMB, R[t], D), x_tile(t, c), tokw[:, c, :],
                              start=(c == 0), stop=(c == CHUNKS - 1))
                last.then_inc(emb_done, 1)

            def turn(t):
                pe.wait_ge(xc_ready, 2 * t + 1)
                if t == 0:
                    pe.wait_ge(cst_loaded, 16)
                if t >= 1:
                    pe.wait_ge(qk_ready, 5 * t)
                nc.tensor.transpose(bank(B_XT, D, R[t]), xc[0:R[t], t, :], ident[0:R[t], 0:R[t]]
                                    ).then_inc(xt_done, 1)

            def project(t):
                cols = xnT[:, OFF[t]:OFF[t] + R[t]]
                pe.wait_ge(xnT_ready, t + 1)
                if t == 0:
                    pe.wait_ge(p65_loaded, 16)
                    pe.wait_ge(pool_setup, filled("wvo"))
                for c in range(4):
                    last = mm(ps[:, B_QK, c * R[t]:(c + 1) * R[t]], wqk[:, c, :], cols, start=True, stop=True)
                last.then_inc(qk_done, 1)
                if t == 0:
                    w_v_w_out()
                    pe.wait_ge(wvo_ready, 1)
                if t >= 1:
                    pe.wait_ge(v_ready, t)
                mm(bank(B_V, R[t], HEADS * D), cols, wvo[:, :], start=True, stop=True).then_inc(v_done, 1)

            def scores(t):
                p = t % 2
                pe.wait_ge(qk_ready, 5 * (t + 1))
                if t == 0:
                    pe.wait_ge(setup_done, 2)
                for c in range(2):
                    if t >= 1:
                        pe.wait_ge(score_read, 2 * (t - 1) + c + 1)
                    out = bank(B_SCORE + c, R[t], 4 * R[t])
                    mm(out.rearrange("p (h n) -> p h n", h=4), farl[:, 0:R[t]], farr[:, :, 0:R[t]],
                       start=True, stop=False)
                    mm(out.rearrange("p (h n) -> p h n", h=4), qT[:, p, c, 0:R[t]], kT[:, p, c, :, 0:R[t]],
                       start=False, stop=True).then_inc(score_done, 1)

            def gram(t):
                r = slice(0, R[t])
                pe.wait_ge(a_ready, 2 * t + 1)
                if t == 0:
                    pe.wait_ge(pool_setup, filled("bd"))
                if t >= 1:
                    pe.wait_ge(gram_read, t)
                mm(bank(B_GRAM, BLOCKS[t], C), const("selw", R[t])[:, 0:BLOCKS[t]],
                   a[r, t].rearrange("p h c -> p (h c)"), start=True, stop=True)
                pe.wait_ge(abd_ready, t + 1)
                for k in range(HEADS):
                    last = parts_product(ps[:, B_GRAM, C + k * ROWS:C + (k + 1) * ROWS], bd[r, t, :, k],
                                         a16[r, t, :, k])
                last.then_inc(gram_done, 1)

            def turn_a(t):
                r = slice(0, R[t])
                for part in range(2):
                    if t >= 1:
                        pe.wait_ge(at_ready, 2 * (t - 1) + part + 1)
                    out16 = ps[:, B_AT + part, :].bitcast(F16).rearrange("p (h n) -> p h n", h=HEADS)
                    for k in range(HEADS):
                        last = nc.tensor.transpose(out16[:, k, 0:R[t]], bd[r, t, part, k, :], ident16[r, r])
                    last.then_inc(at_done, 1)

            def convolution():
                pe.wait_ge(setup_done, 7)
                pe.wait_ge(v_ready, TILES)
                pe.wait_ge(qk_ready, 5 * TILES)
                for k in range(HEADS):
                    last = mm(bank(B_TOEP, RMAX, TILES * D).rearrange("p (t d) -> p t d", t=TILES),
                              toepbd[:, k, :], v[:, :, k * D:(k + 1) * D], start=(k == 0), stop=(k == HEADS - 1))
                last.then_inc(toep_done, 1)

            embed(0)
            for s in range(TILES + 2):
                if s < TILES:
                    turn(s)
                if s + 1 < TILES:
                    embed(s + 1)
                if 1 <= s <= TILES:
                    scores(s - 1)
                if s == TILES + 1:
                    convolution()
                if s >= 2:
                    gram(s - 2)
                    turn_a(s - 2)
                if s < TILES:
                    project(s)
            pe.wait_ge(peak_ready, 1)
            nc.tensor.transpose(bank(B_PEAK, 2, RMAX), peak[:, :], ident[0:RMAX, 0:RMAX]
                                ).then_inc(peakT_done, 1)
            pe.wait_ge(peakd_ready, 1)
            mm(bank(B_PEAK, RMAX, 2), ones2[:, :], peakd[:, :], start=True, stop=True).then_inc(peakb_done, 1)
            pe.wait_ge(at_ready, 2 * TILES)
            pe.wait_ge(pool_setup, filled("bd2"))

            with pe.Fori(0, ITERS) as it:
                for t in range(TILES):
                    r = slice(0, R[t])
                    pe.wait_ge(xbd_ready, it * TILES + (t + 1))
                    pe.wait_ge(xbd_act_ready, it * TILES + (t + 1))
                    for k in range(HEADS):
                        last = parts_product(ps[:, B_ITER(t), k * ROWS:(k + 1) * ROWS],
                                             bd[r, t, :, k], x16[r, t, :, k])
                    last.then_inc(x2_done, 1)
                for t in range(TILES):
                    r = slice(0, R[t])
                    pe.wait_ge(wl_ready, it * TILES + (t + 1))
                    pe.wait_ge(x2bd_ready, it * TILES + (t + 1))
                    pe.wait_ge(x2bd_act_ready, it * TILES + (t + 1))
                    for k in range(HEADS):
                        last = parts_product(ps[:, B_ITER(t), C + k * ROWS:C + (k + 1) * ROWS],
                                             bd2[r, t, :, k], w16[r, t, :, k],
                                             [(bd2[r, t, i, k], eye16[r, :]) for i in range(2)])
                    last.then_inc(prod_done, 1)

            def x_times_v(t):
                r = slice(0, R[t])
                pe.wait_ge(xbd_ready, TILES * ITERS + t + 1)
                pe.wait_ge(xbd_act_ready, TILES * ITERS + t + 1)
                pe.wait_ge(v_cut, t + 1)
                if t >= 2:
                    pe.wait_ge(yvrest_ready, t - 1)
                if t == 1:
                    pe.wait_ge(conv_read, 1)
                for k in range(HEADS):
                    last = parts_product(ps[:, B_YV(t), k * D:(k + 1) * D], bd[r, t, :, k],
                                         v3[r, t, :, k * D:(k + 1) * D])
                last.then_inc(yv_done, 1)

            def a_times(t):
                r = slice(0, R[t])
                pe.wait_ge(yv3_ready, t + 1)
                if t >= 1:
                    pe.wait_ge(h2_read, t)
                if t >= 2:
                    pe.wait_ge(res_ready, t - 1)
                steps = [(k, i) for k in range(HEADS) for i in range(2)]
                for n, (k, i) in enumerate(steps):
                    last = mm(bank(B_ATT, 128, 3 * D).rearrange("p (j d) -> p j d", j=3), aT[r, t, i, k],
                              yv3[r, t % 2, :, k * D:(k + 1) * D], start=(n == 0), stop=(n == len(steps) - 1))
                last.then_inc(att_done, 1)

            def turn_z(t):
                pe.wait_ge(zn_ready, t + 1)
                if t >= 1:
                    pe.wait_ge(pickT_ready, 2 * t)
                nc.tensor.transpose(bank(B_MISC, D, R[t]), zn[0:R[t], t, :], ident[0:R[t], 0:R[t]]
                                    ).then_inc(zt_done, 1)

            def gates(t):
                if t == 0:
                    pe.wait_ge(bias_loaded, 32)
                    pe.wait_ge(ffn_loaded, 32)
                    pe.wait_ge(pool_setup, filled("zT"))
                pe.wait_ge(zT_ready, t + 1)
                mm(bank(B_MISC, R[t], EXPERTS), zT[:, t, 0:R[t]], wg, start=True, stop=True
                   ).then_inc(gate_done, 1)

            def up(t, half):
                if t >= 1:
                    pe.wait_ge(hid_ready, 2 * (t - 1) + half + 1)
                for k in range(4):
                    last = mm(ps[:, B_UP + half, k * R[t]:(k + 1) * R[t]], w1[:, 4 * half + k, :],
                              zT[:, t, 0:R[t]], start=True, stop=True)
                last.then_inc(up_done, 1)

            def turn_picks(t):
                pe.wait_ge(pick_ready, t + 1)
                nc.tensor.transpose(bank(B_MISC, EXPERTS, R[t]), pick[0:R[t], t, :], ident[0:R[t], 0:R[t]]
                                    ).then_inc(pickT_done, 1)

            def picks(t):
                pe.wait_ge(pickT_ready, 2 * t + 1)
                for half in range(2):
                    if t >= 1:
                        pe.wait_ge(hidm_ready, 2 * (t - 1) + half + 1)
                    for k in range(4):
                        last = mm(ps[:, B_PICK + half, k * R[t]:(k + 1) * R[t]], onehot[:, 4 * half + k, :],
                                  pickTb[:, t % 2, 0:R[t]], start=True, stop=True)
                    last.then_inc(pickb_done, 1)

            def down(t):
                out = ps[0:D, B_FFN, AT_FFN:AT_FFN + R[t]]
                pe.wait_ge(h2_read, min(t + 2, TILES))
                mm(out, h2[0:R[t], t, :], ident[0:R[t], 0:R[t]], start=True, stop=False)
                pe.wait_ge(pickT_ready, 2 * t + 2)
                mm(out, b2[:, :], pickT[:, t % 2, 0:R[t]], start=False, stop=False)
                for k in range(EXPERTS):
                    if k % 4 == 0:
                        pe.wait_ge(hidm_ready, 2 * t + k // 4 + 1)
                    last = mm(out, w2[:, k, :], hidm[:, t % 2, k, 0:R[t]], start=False, stop=(k == EXPERTS - 1))
                last.then_inc(ffn_done, 1)

            x_times_v(0)
            x_times_v(1)
            for s in range(1, TILES + 2):
                if s >= 2:
                    gates(s - 2)
                if s == 1:
                    pe.wait_ge(x_ready, (ITERS + 1) * TILES)
                if s <= TILES:
                    a_times(s - 1)
                if s >= 2:
                    up(s - 2, 0)
                    turn_picks(s - 2)
                    up(s - 2, 1)
                    picks(s - 2)
                if s + 1 < TILES:
                    x_times_v(s + 1)
                if s <= TILES:
                    turn_z(s - 1)
                if s >= 2:
                    down(s - 2)


def shape_constants():
    row = np.arange(RMAX)
    image, place = row // ROWS, row % ROWS
    w = np.where(place == 0, np.sqrt(PADS), 1.0)
    wc = np.where(np.arange(ROWS) == 0, np.sqrt(PADS), 1.0)
    parts = {}
    parts["ident"] = np.eye(128)
    parts["blocks"] = image[:, None] == image[None, :]
    parts["wcol"] = np.broadcast_to(wc * wc, (RMAX, ROWS))
    parts["wsym"] = w[:, None] / wc[None, :]
    parts["eye"] = 15.0 / 2.0 * (place[:, None] == np.arange(ROWS))
    parts["selw"] = w[:, None] * (image[:, None] == np.arange(PER_TILE))
    parts["winv"] = np.broadcast_to(1.0 / wc, (RMAX, ROWS))
    parts["before"] = np.broadcast_to(np.tril(np.ones((EXPERTS, EXPERTS)), -1).reshape(1, -1), (RMAX, EXPERTS ** 2))
    farl, farr = np.zeros((128, RMAX)), np.zeros((128, RMAX))
    for j in range(4):
        farl[32 * j] = -FAR / 4
        farr[32 * j] = 1.0
        for g in range(PER_TILE):
            farl[32 * j + 1 + g] = FAR / 4 * (image == g)
            farr[32 * j + 1 + g] = image == g
    parts["farl"], parts["farr"] = farl, farr
    cols, n = starts(CST)
    out = np.zeros((128, n), np.float32)
    for name, (lo, hi) in cols.items():
        out[:len(parts[name]), lo:hi] = parts[name]
    return out


def pack(rows, widths, parts):
    cols, n = starts(widths)
    out = np.zeros((rows, n), np.float32)
    for name, (lo, hi) in cols.items():
        out[:len(parts[name]), lo:hi] = parts[name]
    return out


def kernel(x, L0_tok_W, L0_tok_b, L0_attn_ln_g, L0_attn_ln_b, L0_attn_w_qkv, L0_attn_w_out, L0_attn_b_out,
           L0_attn_res_kernel, L0_ffn_Wg, L0_ffn_bg, L0_ffn_W1, L0_ffn_b1, L0_ffn_W2, L0_ffn_b2):
    import concourse.bacc as bacc
    from concourse.bass_utils import run_bass_kernel_spmd

    x, W, tok_b, g, b, w_qkv, w_out, b_out, rk, Wg, bg, W1, b1, W2, b2 = (np.asarray(i) for i in (
        x, L0_tok_W, L0_tok_b, L0_attn_ln_g, L0_attn_ln_b, L0_attn_w_qkv, L0_attn_w_out, L0_attn_b_out,
        L0_attn_res_kernel, L0_ffn_Wg, L0_ffn_bg, L0_ffn_W1, L0_ffn_b1, L0_ffn_W2, L0_ffn_b2))
    patches = x.reshape(IMAGES, 3, 4, 16, 4, 16).transpose(1, 3, 5, 0, 2, 4).reshape(CHUNKS, 128, IMAGES, TOKENS)
    rows = np.zeros((CHUNKS, 128, IMAGES, ROWS), np.float32)
    rows[..., 1:] = patches
    rows = rows.reshape(CHUNKS, 128, ALL_ROWS).transpose(1, 0, 2)
    x_l = np.concatenate([rows[:, :, OFF[t]:OFF[t] + R[t]].reshape(128, -1) for t in range(TILES)], axis=1)

    wout_bd = np.zeros((2, 4, DH, 4, D), np.float32)
    for j in range(4):
        wout_bd[:, j, :, j, :] = w_out.reshape(2, 4, DH, D)[:, j]
    toep = np.zeros((PER_TILE, ROWS, HEADS, ROWS), np.float32)
    for j in range(TOKENS):
        for i in range(TOKENS):
            toep[:, 1 + j, :, 1 + i] = rk[:, 0, j - i + 16, 0]
    p128 = pack(128, P128, dict(
        tokw=W.T.reshape(CHUNKS, 128, D).transpose(1, 0, 2).reshape(128, -1),
        wvT=w_qkv[:, 2 * HEADS * DH:].T.reshape(2, 128, D).transpose(1, 0, 2).reshape(128, -1),
        woutbd=wout_bd.reshape(2, 128, 4 * D).transpose(1, 0, 2).reshape(128, -1),
        w2=W2.transpose(1, 0, 2).reshape(HIDDEN, -1)))
    p65 = pack(D + 1, P65, dict(
        wqk=w_qkv[:, :2 * HEADS * DH],
        ln=np.stack([g, b], axis=1),
        wg=np.concatenate([Wg, bg[None, :]], axis=0),
        w1=np.concatenate([W1.transpose(1, 0, 2).reshape(D, -1), b1.reshape(1, -1)], axis=0)))
    p119 = pack(RMAX, P119, dict(
        tokb=np.broadcast_to(tok_b, (RMAX, D)), bout=np.broadcast_to(b_out, (RMAX, D)),
        toep=toep.reshape(RMAX, -1)))

    arrays = {"x_l": x_l, "p128": p128, "p65": p65, "p119": p119, "b2": np.ascontiguousarray(b2),
              "cst": shape_constants()}
    nc = bacc.Bacc("TRN2", target_bir_lowering=False, num_devices=1)
    args = [nc.dram_tensor(f"{n}_dram", a.shape, F32, kind="ExternalInput").ap() for n, a in arrays.items()]
    out = nc.dram_tensor("out_dram", [D, ALL_ROWS], F32, kind="ExternalOutput").ap()
    vit_layer(nc, *args, out)
    r = run_bass_kernel_spmd(nc, [{f"{n}_dram": a for n, a in arrays.items()}], core_ids=[0])
    got = r.results[0]["out_dram"]
    return np.ascontiguousarray(got.T.reshape(IMAGES, ROWS, D)[:, 1:, :])
```

```python
from contextlib import ExitStack

import numpy as np

import concourse.bass as bass
from concourse import mybir

F32 = mybir.dt.float32
BF16 = mybir.dt.bfloat16
F16 = mybir.dt.float16
ALU = mybir.AluOpType
ACT = mybir.ActivationFunctionType
AX = mybir.AxisListType.X

IMAGES = 32
TOKENS = 16
PADS = 112
ROWS = TOKENS + 1
PER_TILE = 7
TILES = -(-IMAGES // PER_TILE)
D = 64
HEADS = 8
DH = 32
CHUNKS = 6
EXPERTS = 8
HIDDEN = 128
ITERS = 6
EPS = 1e-5
BLOCKS = [min(PER_TILE, IMAGES - PER_TILE * t) for t in range(TILES)]
R = [ROWS * n for n in BLOCKS]
OFF = [ROWS * PER_TILE * t for t in range(TILES)]
RMAX = R[0]
ALL_ROWS = ROWS * IMAGES
C = HEADS * ROWS
WIDE = 128
ALPHA = 3.5
FAR = float(2.0 ** 100)

P128 = dict(tokw=CHUNKS * D, wvT=2 * D, woutbd=2 * 4 * D, w2=EXPERTS * D)
P65 = dict(wqk=2 * HEADS * DH, ln=2, wg=EXPERTS, w1=EXPERTS * HIDDEN)
P119 = dict(tokb=D, bout=D, toep=C)
CST = dict(ident=128, blocks=RMAX, wcol=ROWS, wsym=ROWS, eye=ROWS, selw=PER_TILE,
           before=EXPERTS * EXPERTS, farl=RMAX, farr=RMAX)


def starts(widths):
    out, at = {}, 0
    for name, w in widths.items():
        out[name] = (at, at + w)
        at += w
    return out, at


def vit_layer(nc, x_in, p128_in, p65_in, p119_in, b2_in, cst_in, out):
    with ExitStack() as ctx:
        def sb(name, shape, dt=F32):
            return ctx.enter_context(nc.sbuf_tensor(name, shape, dt))

        def sem(name):
            return ctx.enter_context(nc.semaphore(name))

        x_sb = sb("x_sb", [128, CHUNKS * ALL_ROWS])
        col128, n128 = starts(P128)
        col65, n65 = starts(P65)
        col119, n119 = starts(P119)
        colc, nc_ = starts(CST)
        p128 = sb("p128", [128, n128])
        p65 = sb("p65", [128, n65])
        p119 = sb("p119", [RMAX, n119])
        b2 = sb("b2", [128, D])
        cst = sb("cst", [128, nc_])

        def v128(name):
            return p128[:, col128[name][0]:col128[name][1]]

        def v65(name, rows=D):
            return p65[0:rows, col65[name][0]:col65[name][1]]

        def v119(name):
            return p119[:, col119[name][0]:col119[name][1]]

        def const(name, rows=128):
            return cst[0:rows, colc[name][0]:colc[name][1]]

        tokw = v128("tokw").rearrange("p (c e) -> p c e", c=CHUNKS)
        wvT = v128("wvT").rearrange("p (c e) -> p c e", c=2)
        woutbd = v128("woutbd").rearrange("p (c n) -> p c n", c=2)
        w2 = v128("w2").rearrange("p (e d) -> p e d", e=EXPERTS)
        wqk = v65("wqk", 128).rearrange("p (c m) -> p c m", c=4)
        wg = v65("wg", 128)
        w1 = v65("w1", 128).rearrange("p (e h) -> p e h", e=EXPERTS)
        toep = v119("toep").rearrange("p (h c) -> p h c", h=HEADS)
        ident = const("ident")

        h = sb("h", [RMAX, TILES, D])
        base = sb("base", [RMAX, TILES, D])
        h2 = sb("h2", [RMAX, TILES, D])
        conv = sb("conv", [RMAX, TILES, D])
        att = sb("att", [RMAX, D])
        res = sb("res", [RMAX, TILES, D])
        stats = sb("stats", [RMAX, TILES, 6])
        moments = sb("moments", [RMAX, TILES, 2])
        powarg = sb("powarg", [RMAX, TILES, 2])
        rstd = sb("rstd", [RMAX, TILES, 2])
        exponent = sb("exponent", [RMAX, 2])
        zero = sb("zero", [RMAX, HEADS])
        warm = sb("warm", [RMAX, 2])
        xc = sb("xc", [RMAX, TILES, D])
        xnT = sb("xnT", [128, ALL_ROWS])
        qT = sb("qT", [128, 2, 2, RMAX])
        kT = sb("kT", [128, 2, 2, 4, RMAX])
        wvo = sb("wvo", [128, HEADS * D])
        v = sb("v", [RMAX, TILES, HEADS * D])
        score = sb("score", [RMAX, 2, HEADS, ROWS])
        smax = sb("smax", [RMAX, 2, HEADS])
        e = sb("e", [RMAX, 2, HEADS, ROWS])
        z = sb("z", [RMAX, 2, HEADS])
        rz = sb("rz", [RMAX, 2, HEADS])
        a = sb("a", [RMAX, TILES, HEADS, ROWS])
        peaks = sb("peaks", [RMAX, 2, TILES])
        colw = sb("colw", [PER_TILE, TILES, HEADS, ROWS])
        peak = sb("peak", [RMAX, 2])
        peak2 = sb("peak2", [2, 1])
        peakd = sb("peakd", [2, 2])
        scale = sb("scale", [RMAX, 1])
        rscale = sb("rscale", [RMAX, 1])
        ones2 = sb("ones2", [2, RMAX])
        bd = sb("bd", [RMAX, TILES, 2, HEADS, WIDE], F16)
        bd2 = sb("bd2", [RMAX, TILES, 2, HEADS, WIDE], F16)
        aT = sb("aT", [RMAX, TILES, 2, HEADS, WIDE], F16)
        a16 = sb("a16", [RMAX, TILES, 2, HEADS, ROWS], F16)
        x16 = sb("x16", [RMAX, TILES, 2, HEADS, ROWS], F16)
        x2_16 = sb("x2_16", [RMAX, TILES, 2, HEADS, ROWS], F16)
        w16 = sb("w16", [RMAX, TILES, 2, HEADS, ROWS], F16)
        blocks16 = sb("blocks16", [RMAX, RMAX], F16)
        ident16 = sb("ident16", [128, 128], F16)
        v3 = sb("v3", [RMAX, TILES, 3, HEADS * D], BF16)
        vrest = sb("vrest", [RMAX, 2, HEADS * D])
        toepbd = sb("toepbd", [RMAX, HEADS, RMAX])
        xm = sb("xm", [RMAX, TILES, HEADS, ROWS])
        xe = sb("xe", [RMAX, TILES, HEADS, ROWS])
        xw = sb("xw", [RMAX, TILES, HEADS, ROWS])
        yv3 = sb("yv3", [RMAX, 2, 3, HEADS * D], BF16)
        yvrest = sb("yvrest", [RMAX, 2, HEADS * D])
        farl = sb("farl", [128, RMAX], BF16)
        farr = sb("farr", [128, 4, RMAX], BF16)
        zn = sb("zn", [RMAX, TILES, D])
        zT = sb("zT", [128, TILES, RMAX])
        gate = sb("gate", [RMAX, EXPERTS])
        ahead = sb("ahead", [RMAX, 2, EXPERTS, EXPERTS])
        rank = sb("rank", [RMAX, EXPERTS])
        pick = sb("pick", [RMAX, TILES, EXPERTS])
        pickT = sb("pickT", [128, 2, RMAX])
        pickTb = sb("pickTb", [128, 2, RMAX], BF16)
        onehot = sb("onehot", [128, EXPERTS, HIDDEN], BF16)
        hid = sb("hid", [HIDDEN, 2, EXPERTS, RMAX])
        hidm = sb("hidm", [HIDDEN, 2, EXPERTS, RMAX])

        ps = ctx.enter_context(nc.psum_tensor("ps", [128, 8, 512], F32))

        def bank(b, rows, cols):
            return ps[0:rows, b, 0:cols]

        B_EMB, B_K, B_V = 0, 1, 2
        B_COLS, AT_COLS = 0, D
        B_SCORE = 3
        B_XT, B_GRAM, B_Q, AT_Q = 5, 5, 5, 256
        B_AT = 6
        B_WVO, B_PEAK, B_TOEP, B_IDLE = 3, 0, 1, 7
        def B_ITER(t): return 2 + t
        def B_YV(t): return t % 2
        def B_FFN(t): return t % 2
        B_ATT, B_MISC, B_UP, B_PICK = 2, 3, 4, 6

        x_in_sem = [sem(f"x_loaded{t}") for t in range(TILES)]
        tokw_loaded, wv_loaded, p65_loaded = sem("tokw_loaded"), sem("wv_loaded"), sem("p65_loaded")
        p119_loaded, cst_loaded, ffn_loaded = sem("p119_loaded"), sem("cst_loaded"), sem("ffn_loaded")
        bias_loaded, tokb_loaded = sem("bias_loaded"), sem("tokb_loaded")
        stored = sem("stored")
        wvo_done, emb_done, xt_done, k_done, q_done, v_done = (sem(n) for n in (
            "wvo_done", "emb_done", "xt_done", "k_done", "q_done", "v_done"))
        score_done, cols_done, gram_done, at_done = (sem(n) for n in (
            "score_done", "cols_done", "gram_done", "at_done"))
        toep_done, peakT_done, peakb_done = sem("toep_done"), sem("peakT_done"), sem("peakb_done")
        x2_done, prod_done = sem("x2_done"), sem("prod_done")
        yv_done, att_done, zt_done, gate_done = (sem(n) for n in ("yv_done", "att_done", "zt_done", "gate_done"))
        up_done, pickT_done, pickb_done, ffn_done = (sem(n) for n in (
            "up_done", "pickT_done", "pickb_done", "ffn_done"))
        dve_step = sem("dve_step")
        setup_done, choose_step = sem("setup_done"), sem("choose_step")
        emb_read, arg_ready, xc_ready = sem("emb_read"), sem("arg_ready"), sem("xc_ready")
        score_ready, score_read = sem("score_ready"), sem("score_read")
        a_ready, abd_ready = sem("a_ready"), sem("abd_ready")
        peak_ready, peakd_ready = sem("peak_ready"), sem("peakd_ready")
        ah_ready = sem("ah_ready")
        al_ready = sem("al_ready")
        x_ready, xbd_ready, w_ready, x2l_ready, x2bd_ready = (sem(n) for n in (
            "x_ready", "xbd_ready", "w_ready", "x2l_ready", "x2bd_ready"))
        yvrest_ready = sem("yvrest_ready")
        yv3_ready = sem("yv3_ready")
        h2_read, arg2_ready, zn_ready = sem("h2_read"), sem("arg2_ready"), sem("zn_ready")
        gate_read, pick_ready, hidm_ready, res_ready = (sem(n) for n in (
            "gate_read", "pick_ready", "hidm_ready", "res_ready"))
        wvo_ready, xnT_ready, qk_ready, v_ready, e_ready = (sem(n) for n in (
            "wvo_ready", "xnT_ready", "qk_ready", "v_ready", "e_ready"))
        cols_ready, gram_read, at_ready = sem("cols_ready"), sem("gram_read"), sem("at_ready")
        zT_ready, hid_ready, pickT_ready = sem("zT_ready"), sem("hid_ready"), sem("pickT_ready")
        xh_ready, x2h_ready = sem("xh_ready"), sem("x2h_ready")
        abd_act_ready, xbd_act_ready, x2bd_act_ready = (sem(n) for n in (
            "abd_act_ready", "xbd_act_ready", "x2bd_act_ready"))
        conv_read = sem("conv_read")
        yv1_ready, yv2_ready = sem("yv1_ready"), sem("yv2_ready")
        xe_ready, wh_ready = sem("xe_ready"), sem("wh_ready")
        xl_ready, wl_ready = sem("xl_ready"), sem("wl_ready")
        base_complete = sem("base_complete")
        v_cut, v_cut_step = sem("v_cut"), sem("v_cut_step")
        pool_setup, rstd_ready, rstd2_ready, base_ready, base_step = (sem(n) for n in (
            "pool_setup", "rstd_ready", "rstd2_ready", "base_ready", "base_step"))

        def x_tile(t, c):
            at = CHUNKS * OFF[t] + c * R[t]
            return x_sb[:, at:at + R[t]]

        def blocks(t, ap):
            return ap[:, :, None, :].broadcast_to([R[t], ap.shape[1], BLOCKS[t], ROWS])

        def mask(t, heads=HEADS):
            m = const("blocks", R[t])[:, 0:R[t]].rearrange("p (g c) -> p g c", c=ROWS)
            return m[:, None, :, :].broadcast_to([R[t], heads, BLOCKS[t], ROWS])

        def spread(engine_tt, dst, src, t, n):
            r = slice(0, R[t])
            shape = [R[t], 2 * HEADS, n, ROWS]
            m = blocks16[r, 0:n * ROWS].rearrange("p (g c) -> p g c", c=ROWS)
            return engine_tt(
                dst[r, t, :, :, 0:n * ROWS].rearrange("p s h (g c) -> p (s h) g c", c=ROWS),
                src[r, t].rearrange("p s h c -> p (s h) c")[:, :, None, :].broadcast_to(shape),
                m[:, None, :, :].broadcast_to(shape), ALU.mult)

        def by_image(ap):
            return ap.rearrange("p h (g c) -> p h g c", c=ROWS)

        ACT_BLOCKS = [2] * (TILES - 1) + [1]
        block = ctx.enter_context(nc.Block())

        fills = [("exponent", exponent[:], -0.5), ("xnT", xnT[:], 0.0), ("p65", p65[D:, :], 0.0),
                 ("wvo", wvo[D:, :], 0.0), ("kT", kT[:], 0.0),
                 ("peaks", peaks[:], 0.0), ("ones2", ones2[:], 1.0), ("zero", zero[:], 0.0),
                 ("bd", bd[:, 0:TILES - 1, :, :, RMAX:], 0.0), ("bd", bd[:, TILES - 1, :, :, R[-1]:], 0.0),
                 ("b2", b2[:], 0.0), ("pickT", pickT[:], 0.0), ("pickTb", pickTb[:], 0.0),
                 ("aT", aT[:, 0:TILES - 1, :, :, RMAX:], 0.0), ("aT", aT[:, TILES - 1, :, :, R[-1]:], 0.0),
                 ("zT", zT[D:, :, :], 0.0), ("zT", zT[D:D + 1, :, :], 1.0),
                 ("v", v[64:RMAX, TILES - 1, :], 0.0), ("base", base[64:RMAX, TILES - 1, :], 0.0),
                 ("bd2", bd2[:, 0:TILES - 1, :, :, RMAX:], 0.0), ("bd2", bd2[:, TILES - 1, :, :, R[-1]:], 0.0)]

        def filled(name):
            return max(n + 1 for n, fill in enumerate(fills) if fill[0] == name)

        @block.sync
        def _(sp):
            sp.dma_start(p128[:, 0:CHUNKS * D], p128_in[:, 0:CHUNKS * D]).then_inc(tokw_loaded, 16)
            for t in range(TILES):
                cols = slice(CHUNKS * OFF[t], CHUNKS * (OFF[t] + R[t]))
                sp.dma_start(x_sb[:, cols], x_in[:, cols]).then_inc(x_in_sem[t], 16)
            sp.dma_start(p119[:, D:], p119_in[:, D:]).then_inc(p119_loaded, 16)
            sp.dma_start(p65[0:D, col65["w1"][0]:], p65_in[0:D, col65["w1"][0]:]).then_inc(ffn_loaded, 16)
            sp.dma_start(p128[:, col128["w2"][0]:], p128_in[:, col128["w2"][0]:]).then_inc(ffn_loaded, 16)
            sp.wait_ge(pool_setup, filled("p65"))
            bias_row = slice(col65["wg"][0], n65)
            sp.dma_start(p65[D:D + 1, bias_row], p65_in[D:D + 1, bias_row]).then_inc(bias_loaded, 16)
            sp.wait_ge(pool_setup, filled("b2"))
            sp.dma_start(b2[0:EXPERTS, :], b2_in).then_inc(bias_loaded, 16)
            for t in range(TILES):
                sp.wait_ge(res_ready, t + 1)
                sp.dma_start(out[OFF[t]:OFF[t] + R[t], :], res[0:R[t], t, :]).then_inc(stored, 16)
            sp.wait_ge(stored, 16 * TILES)

        @block.gpsimd
        def _(pool):
            def fill(n):
                if n:
                    pool.wait_ge(pool_setup, n)
                nc.gpsimd.memset(fills[n][1], fills[n][2]).then_inc(pool_setup, 1)

            def rstd_of(t):
                r = slice(0, R[t])
                pool.wait_ge(arg_ready, 2 * (t + 1))
                nc.gpsimd.tensor_tensor(rstd[r, t, :], powarg[r, t, :], exponent[r, :],
                                        ALU.pow).then_inc(rstd_ready, 1)

            group_ends = [filled("pickTb"), filled("zT"), len(fills)]
            for n in range(group_ends[0]):
                fill(n)

            def base_of(t):
                r = slice(0, R[t])
                if t == 0:
                    pool.wait_ge(p119_loaded, 16)
                pool.wait_ge(xc_ready, 2 * (t + 1))
                nc.gpsimd.tensor_tensor(base[r, t, :], h[r, t, :], v119("bout")[r, :],
                                        ALU.add).then_inc(base_step, 1)
                pool.wait_ge(base_step, t + 1)
                nc.gpsimd.tensor_tensor(base[r, t, :], base[r, t, :], h2[r, t, :],
                                        ALU.add).then_inc(base_ready, 1)

            def cut_v(t):
                r = slice(0, R[t])
                no_v = zero[r, 0:1].broadcast_to([R[t], HEADS * D])
                pool.wait_ge(v_ready, t + 1)
                nc.gpsimd.tensor_tensor(v3[r, t, 0], v[r, t], no_v, ALU.add).then_inc(v_cut_step, 1)
                pool.wait_ge(v_cut_step, 3 * t + 1)
                nc.gpsimd.tensor_tensor(vrest[r, t % 2], v[r, t], v3[r, t, 0], ALU.subtract).then_inc(v_cut_step, 1)
                pool.wait_ge(v_cut_step, 3 * t + 2)
                nc.gpsimd.tensor_tensor(v3[r, t, 1], vrest[r, t % 2], no_v, ALU.add).then_inc(v_cut_step, 1)
                pool.wait_ge(v_cut_step, 3 * t + 3)
                nc.gpsimd.tensor_tensor(v3[r, t, 2], vrest[r, t % 2], v3[r, t, 1], ALU.subtract).then_inc(v_cut, 1)

            pool.wait_ge(pool_setup, group_ends[0])
            rstd_of(0)
            for s in range(TILES + 1):
                if s + 1 < len(group_ends):
                    pool.wait_ge(rstd_ready, s + 1)
                    for n in range(group_ends[s], group_ends[s + 1]):
                        fill(n)
                    pool.wait_ge(pool_setup, group_ends[s + 1])
                if s + 1 < TILES:
                    rstd_of(s + 1)
                if s >= 1:
                    cut_v(s - 1)
                    base_of(s - 1)

            def second_x(t, count):
                pool.wait_ge(xh_ready, count)
                nc.gpsimd.tensor_tensor(x16[0:R[t], t, 1], xm[0:R[t], t], x16[0:R[t], t, 0], ALU.subtract
                                        ).then_inc(xl_ready, 1)

            def less_eye(t):
                eye = const("eye", R[t])[:, None, :].broadcast_to([R[t], HEADS, ROWS])
                nc.gpsimd.tensor_tensor(xe[0:R[t], t], xm[0:R[t], t], eye, ALU.subtract).then_inc(xe_ready, 1)

            for t in range(TILES):
                second_x(t, t + 1)
                less_eye(t)
            with pool.Fori(0, ITERS) as it:
                for t in range(TILES):
                    pool.wait_ge(w_ready, it * TILES + (t + 1))
                    nc.gpsimd.tensor_tensor(w16[0:R[t], t, 0], xw[0:R[t], t],
                                            zero[0:R[t], :, None].broadcast_to([R[t], HEADS, ROWS]), ALU.add
                                            ).then_inc(wh_ready, 1)
                    pool.wait_ge(wh_ready, it * TILES + (t + 1))
                    nc.gpsimd.tensor_tensor(w16[0:R[t], t, 1], xw[0:R[t], t], w16[0:R[t], t, 0], ALU.subtract
                                            ).then_inc(wl_ready, 1)
                for t in range(TILES):
                    second_x(t, it * TILES + (TILES + t + 1))
                    less_eye(t)
            pool.wait_ge(conv_read, 1)
            pool.wait_ge(base_ready, TILES)
            nc.gpsimd.tensor_tensor(base[:, :, :], base[:, :, :], conv[:, :, :], ALU.add).then_inc(base_complete, 1)

            def third_yv(t):
                r, p = slice(0, R[t]), t % 2
                pool.wait_ge(yv2_ready, t + 1)
                nc.gpsimd.tensor_tensor(yv3[r, p, 2], yvrest[r, p], yv3[r, p, 1], ALU.subtract
                                        ).then_inc(yv3_ready, 1)

            pool.wait_ge(yv3_ready, 1)
            third_yv(1)
            for t in range(TILES):
                r = slice(0, R[t])
                pool.wait_ge(arg2_ready, t + 1)
                nc.gpsimd.tensor_tensor(rstd[r, t, 0:1], powarg[r, t, 0:1], exponent[r, 0:1],
                                        ALU.pow).then_inc(rstd2_ready, 1)
                if t + 2 < TILES:
                    third_yv(t + 2)

        @block.scalar
        def _(act):
            act.dma_start(p119[:, 0:D], p119_in[:, 0:D]).then_inc(tokb_loaded, 16)
            act.dma_start(cst[:, :], cst_in).then_inc(cst_loaded, 16)
            early = slice(0, col65["w1"][0])
            act.dma_start(p65[0:D, early], p65_in[0:D, early]).then_inc(p65_loaded, 16)
            wv = slice(col128["wvT"][0], col128["w2"][0])
            act.dma_start(p128[:, wv], p128_in[:, wv]).then_inc(wv_loaded, 16)
            ln = v65("ln")
            act.wait_ge(pool_setup, filled("exponent"))
            nc.scalar.activation(warm[:, :], exponent[:, :], ACT.Exp)

            def turned(t):
                if t == 0:
                    act.wait_ge(p65_loaded, 16)
                    act.wait_ge(pool_setup, filled("xnT"))
                act.wait_ge(xt_done, t + 1)
                cols = slice(OFF[t], OFF[t] + R[t])
                nc.scalar.activation(
                    xnT[0:D, cols].rearrange("p (n s) -> p n s", s=ROWS)[:, :, 1:ROWS],
                    bank(B_XT, D, R[t]).rearrange("p (n s) -> p n s", s=ROWS)[:, :, 1:ROWS],
                    ACT.Identity, bias=ln[:, 1:2], scale=ln[:, 0:1]).then_inc(xnT_ready, 1)

            def q_k_out(t):
                p = t % 2
                if t == 0:
                    act.wait_ge(pool_setup, filled("kT"))
                act.wait_ge(k_done, t + 1)
                if t >= 2:
                    act.wait_ge(score_done, 2 * (t - 1))
                for j in range(4):
                    rows = slice(DH * j, DH * j + DH)
                    nc.scalar.copy(kT[rows, p, :, j, 0:R[t]],
                                   bank(B_K, 128, 2 * R[t])[rows].rearrange("p (c n) -> p c n", c=2)
                                   ).then_inc(qk_ready, 1)
                act.wait_ge(q_done, t + 1)
                nc.scalar.activation(qT[:, p, :, 0:R[t]],
                                     ps[:, B_Q, AT_Q:AT_Q + 2 * R[t]].rearrange("p (c n) -> p c n", c=2),
                                     ACT.Copy, scale=DH ** -0.5).then_inc(qk_ready, 1)

            def v_out(t):
                r = slice(0, R[t])
                if t == TILES - 1:
                    act.wait_ge(pool_setup, filled("v"))
                act.wait_ge(v_done, t + 1)
                nc.scalar.copy(v[r, t, :], bank(B_V, R[t], HEADS * D)).then_inc(v_ready, 1)

            def softmax_exp(t):
                act.wait_ge(score_ready, t + 1)
                nc.scalar.activation(e[0:R[t], t % 2], score[0:R[t], t % 2], ACT.Exp).then_inc(e_ready, 1)

            def spread_last(dst, src, t):
                r = slice(0, R[t])
                for g in range(BLOCKS[t] - ACT_BLOCKS[t], BLOCKS[t]):
                    last = nc.scalar.activation(
                        dst[r, t, :, :, ROWS * g:ROWS * g + ROWS].rearrange("p s h c -> p (s h) c"),
                        src[r, t].rearrange("p s h c -> p (s h) c"), ACT.Copy,
                        scale=const("blocks", R[t])[:, ROWS * g:ROWS * g + 1])
                return last

            def spread_a(t):
                if t == 0:
                    act.wait_ge(cst_loaded, 16)
                act.wait_ge(al_ready, t + 1)
                spread_last(bd, a16, t).then_inc(abd_act_ready, 1)

            def columns_out(t):
                act.wait_ge(cols_done, t + 1)
                nc.scalar.copy(colw[0:BLOCKS[t], t], ps[0:BLOCKS[t], B_COLS, AT_COLS:AT_COLS + C].rearrange(
                    "p (h c) -> p h c", c=ROWS)).then_inc(cols_ready, 1)

            def gram_out(t):
                act.wait_ge(gram_done, t + 1)
                nc.scalar.copy(xm[0:R[t], t], bank(B_GRAM, R[t], C).rearrange(
                    "p (h c) -> p h c", c=ROWS)).then_inc(gram_read, 1)

            def turned_a(t, part):
                if t == 0 and part == 0:
                    act.wait_ge(pool_setup, filled("aT"))
                act.wait_ge(at_done, 2 * t + part + 1)
                nc.scalar.copy(aT[0:R[t], t, part, :, 0:R[t]],
                               ps[0:R[t], B_AT + part, :].bitcast(F16).rearrange("p (h n) -> p h n", h=HEADS)[:, :, 0:R[t]]
                               ).then_inc(at_ready, 1)

            act.wait_ge(pool_setup, filled("wvo"))
            act.wait_ge(wvo_done, 1)
            nc.scalar.copy(wvo[0:D, :], bank(B_WVO, D, HEADS * D)).then_inc(wvo_ready, 1)
            for s in range(TILES + 2):
                if s < TILES:
                    turned(s)
                if s >= 2:
                    spread_a(s - 2)
                if 1 <= s <= TILES:
                    softmax_exp(s - 1)
                if s >= 2:
                    columns_out(s - 2)
                    gram_out(s - 2)
                    turned_a(s - 2, 0)
                if s < TILES:
                    q_k_out(s)
                if s >= 2:
                    turned_a(s - 2, 1)
                if s < TILES:
                    v_out(s)

            def first_x(t, count):
                act.wait_ge(x_ready, count)
                nc.scalar.copy(x16[0:R[t], t, 0], xm[0:R[t], t]).then_inc(xh_ready, 1)

            def spread_x(t, count):
                act.wait_ge(xl_ready, count)
                spread_last(bd, x16, t).then_inc(xbd_act_ready, 1)

            def first_x2(t, count):
                r = slice(0, R[t])
                act.wait_ge(w_ready, count)
                nc.scalar.activation(x2_16[r, t, 0], ps[r, B_ITER(t), 0:C].rearrange("p (h c) -> p h c", c=ROWS),
                                     ACT.Copy, scale=-1.0 / 7.0).then_inc(x2h_ready, 1)

            def spread_x2(t, count):
                act.wait_ge(x2l_ready, count)
                spread_last(bd2, x2_16, t).then_inc(x2bd_act_ready, 1)

            for t in range(TILES):
                first_x(t, t + 1)
                if t >= 1:
                    spread_x(t - 1, t)
            act.wait_ge(toep_done, 1)
            nc.scalar.copy(conv[:, :, :], bank(B_TOEP, RMAX, TILES * D).rearrange("p (t d) -> p t d", t=TILES)
                           ).then_inc(conv_read, 1)
            with act.Fori(0, ITERS) as it:
                for t in range(TILES):
                    first_x2(t, it * TILES + (t + 1))
                    if t == 0:
                        spread_x(TILES - 1, it * TILES + TILES)
                    else:
                        spread_x2(t - 1, it * TILES + t)
                for t in range(TILES):
                    first_x(t, it * TILES + (TILES + t + 1))
                    if t == 0:
                        spread_x2(TILES - 1, it * TILES + TILES)
                    else:
                        spread_x(t - 1, it * TILES + (TILES + t))

            def first_yv(t):
                act.wait_ge(yv_done, t + 1)
                if t >= 2:
                    act.wait_ge(att_done, t - 1)
                nc.scalar.activation(yv3[0:R[t], t % 2, 0], bank(B_YV(t), R[t], HEADS * D), ACT.Copy,
                                     scale=1.0 / ALPHA).then_inc(yv1_ready, 1)

            def second_yv(t):
                act.wait_ge(yvrest_ready, t + 1)
                nc.scalar.copy(yv3[0:R[t], t % 2, 1], yvrest[0:R[t], t % 2]).then_inc(yv2_ready, 1)

            def gelu(t, half):
                act.wait_ge(up_done, 2 * t + half + 1)
                if t >= 2 and half == 0:
                    act.wait_ge(hidm_ready, 2 * (t - 1))
                nc.scalar.activation(hid[:, t % 2, 4 * half:4 * half + 4, 0:R[t]],
                                     bank(B_UP + half, HIDDEN, 4 * R[t]).rearrange("p (e n) -> p e n", e=4),
                                     ACT.Gelu).then_inc(hid_ready, 1)

            def pick_out(t):
                p = t % 2
                act.wait_ge(pickT_done, t + 1)
                if t >= 2:
                    act.wait_ge(ffn_done, t - 1)
                src = bank(B_MISC, EXPERTS, R[t])
                nc.scalar.copy(pickTb[0:EXPERTS, p, 0:R[t]], src).then_inc(pickT_ready, 1)
                nc.scalar.copy(pickT[0:EXPERTS, p, 0:R[t]], src).then_inc(pickT_ready, 1)

            def z_out(t):
                act.wait_ge(zt_done, t + 1)
                nc.scalar.copy(zT[0:D, t, 0:R[t]], bank(B_MISC, D, R[t])).then_inc(zT_ready, 1)

            first_yv(0)
            second_yv(0)
            spread_x(TILES - 1, (ITERS + 1) * TILES)
            first_yv(1)
            second_yv(1)
            nc.scalar.activation(warm[:, :], exponent[:, :], ACT.Gelu)
            for s in range(1, TILES + 2):
                if s >= 2:
                    gelu(s - 2, 0)
                    pick_out(s - 2)
                    gelu(s - 2, 1)
                if s + 1 < TILES:
                    first_yv(s + 1)
                if s <= TILES:
                    z_out(s - 1)
                if s + 1 < TILES:
                    second_yv(s + 1)

        @block.vector
        def _(dve):
            steps = [0]

            def own(instruction):
                steps[0] += 1
                instruction.then_inc(dve_step, 1)
                dve.wait_ge(dve_step, steps[0])

            tt, ts, stt = nc.vector.tensor_tensor, nc.vector.tensor_scalar, nc.vector.scalar_tensor_tensor
            def layernorm_stats(t, src):
                r = slice(0, R[t])
                own(nc.vector.bn_stats(stats[r, t, :], src))
                own(nc.vector.bn_aggr(moments[r, t, :], stats[r, t, :]))

            def masks():
                dve.wait_ge(cst_loaded, 16)
                nc.vector.tensor_copy(farl[:, :], const("farl")).then_inc(setup_done, 1)
                nc.vector.tensor_copy(farr[:, :, :], const("farr")[:, None, :].broadcast_to([128, 4, RMAX])
                                      ).then_inc(setup_done, 1)
                nc.vector.tensor_copy(blocks16[:, :], const("blocks", RMAX)).then_inc(setup_done, 1)
                nc.vector.tensor_copy(ident16[:, :], ident).then_inc(setup_done, 1)

            def other_constants():
                nc.vector.tensor_copy(onehot[:, :, :],
                                      ident[:, 0:EXPERTS][:, :, None].broadcast_to([128, EXPERTS, HIDDEN])).then_inc(setup_done, 1)
                dve.wait_ge(p119_loaded, 16)
                tt(by_image(toepbd[:, :, :]), blocks(0, toep), mask(0), ALU.mult).then_inc(setup_done, 1)

            def embed(t):
                r = slice(0, R[t])
                if t == 0:
                    dve.wait_ge(tokb_loaded, 16)
                dve.wait_ge(emb_done, t + 1)
                tt(h[r, t, :], bank(B_EMB, R[t], D), v119("tokb")[r, :], ALU.add).then_inc(emb_read, 1)
                dve.wait_ge(emb_read, t + 1)
                layernorm_stats(t, h[r, t, :])
                ts(powarg[r, t, 0:1], moments[r, t, 1:2], EPS, None, ALU.add).then_inc(arg_ready, 1)
                ts(powarg[r, t, 1:2], moments[r, t, 1:2], 1.0 + EPS, EPS * EPS, ALU.mult, ALU.add
                   ).then_inc(arg_ready, 1)

            def normalise(t):
                r = slice(0, R[t])
                dve.wait_ge(rstd_ready, t + 1)
                ts(xc[r, t, :], h[r, t, :], moments[r, t, 0:1], rstd[r, t, 1:2], ALU.subtract, ALU.mult
                   ).then_inc(xc_ready, 1)
                ts(h2[r, t, :], h[r, t, :], moments[r, t, 0:1], rstd[r, t, 0:1], ALU.subtract, ALU.mult
                   ).then_inc(xc_ready, 1)

            def scores_out(t):
                r = slice(0, R[t])
                p = t % 2
                if t >= 2:
                    dve.wait_ge(e_ready, t - 1)
                for c in range(2):
                    dve.wait_ge(score_done, 2 * t + c + 1)
                    nc.vector.tensor_reduce(
                        score[r, p, 4 * c:4 * c + 4, :],
                        bank(B_SCORE + c, R[t], 4 * R[t]).rearrange("p (h g c) -> p h c g", h=4, c=ROWS),
                        AX, ALU.max).then_inc(score_read, 1)
                dve.wait_ge(score_read, 2 * (t + 1))
                own(nc.vector.tensor_reduce(smax[r, p, :], score[r, p], AX, ALU.max))
                tt(score[r, p], score[r, p], smax[r, p, :, None].broadcast_to([R[t], HEADS, ROWS]),
                   ALU.subtract).then_inc(score_ready, 1)

            def softmax(t):
                r = slice(0, R[t])
                p = t % 2
                wcol = const("wcol", R[t])[:, None, :].broadcast_to([R[t], HEADS, ROWS])
                wsym = const("wsym", R[t])[:, None, :].broadcast_to([R[t], HEADS, ROWS])
                dve.wait_ge(e_ready, t + 1)
                own(tt(e[r, p], e[r, p], wcol, ALU.mult))
                own(nc.vector.tensor_reduce(z[r, p, :], e[r, p], AX, ALU.add))
                own(nc.vector.reciprocal(rz[r, p, :], z[r, p, :]))
                own(tt(e[r, p], e[r, p], rz[r, p, :, None].broadcast_to([R[t], HEADS, ROWS]), ALU.mult))
                tt(a[r, t], e[r, p], wsym, ALU.mult).then_inc(a_ready, 1)
                own(nc.vector.tensor_reduce(z[r, p, :], e[r, p], AX, ALU.add))
                dve.wait_ge(a_ready, 2 * t + 1)
                nc.vector.tensor_copy(a16[r, t, 0], a[r, t]).then_inc(ah_ready, 1)
                nc.vector.tensor_reduce(peaks[r, 0, t:t + 1], z[r, p, :], AX, ALU.max).then_inc(a_ready, 1)

            def spread_a(t):
                r = slice(0, R[t])
                if t == 0:
                    dve.wait_ge(setup_done, 4)
                dve.wait_ge(ah_ready, t + 1)
                tt(a16[r, t, 1], a[r, t], a16[r, t, 0], ALU.subtract).then_inc(al_ready, 1)
                dve.wait_ge(al_ready, t + 1)
                spread(tt, bd, a16, t, BLOCKS[t] - ACT_BLOCKS[t]).then_inc(abd_ready, 1)

            def column_peaks(tiles, rows):
                n = len(tiles)
                t0 = tiles[0]
                pads = colw[0:rows, t0:t0 + n, :, 0:1].rearrange("p t h c -> p (t h) c")
                own(ts(pads, pads, PADS ** -0.5, None, ALU.mult))
                own(nc.vector.tensor_reduce(peaks[0:rows, 1, t0:t0 + n],
                                            colw[0:rows, t0:t0 + n].rearrange("p t h c -> p t (h c)"),
                                            AX, ALU.max))

            embed(0)
            masks()
            normalise(0)
            for s in range(TILES + 2):
                if s >= 2:
                    spread_a(s - 2)
                if s + 1 < TILES:
                    embed(s + 1)
                if 1 <= s <= TILES:
                    scores_out(s - 1)
                if s + 1 < TILES:
                    normalise(s + 1)
                if s == 0:
                    other_constants()
                if 1 <= s <= TILES:
                    if s == 1:
                        dve.wait_ge(pool_setup, filled("peaks"))
                    softmax(s - 1)

            dve.wait_ge(cols_ready, TILES - 1)
            dve.wait_ge(a_ready, 2 * TILES)
            column_peaks(range(TILES - 1), PER_TILE)
            dve.wait_ge(cols_ready, TILES)
            column_peaks([TILES - 1], BLOCKS[-1])
            nc.vector.tensor_reduce(peak[:, :], peaks[:, :, :], AX, ALU.max).then_inc(peak_ready, 1)
            dve.wait_ge(peakT_done, 1)
            own(nc.vector.tensor_reduce(peak2[:, :], bank(B_PEAK, 2, RMAX), AX, ALU.max))
            ts(peakd[:, :], ident[0:2, 0:2], peak2[:, 0:1], None, ALU.mult).then_inc(peakd_ready, 1)
            dve.wait_ge(peakb_done, 1)
            own(nc.vector.tensor_reduce(scale[:, :], bank(B_PEAK, RMAX, 2), AX, ALU.mult))
            own(nc.vector.reciprocal(rscale[:, :], scale[:, :]))

            def new_x(t, count):
                r = slice(0, R[t])
                prod = ps[r, B_ITER(t), C:2 * C].rearrange("p (h c) -> p h c", c=ROWS)
                dve.wait_ge(prod_done, count)
                stt(xm[r, t], xm[r, t], 13.0 / 4.0, prod, ALU.mult, ALU.add).then_inc(x_ready, 1)

            def spread_x(t, count):
                dve.wait_ge(xl_ready, count)
                spread(tt, bd, x16, t, BLOCKS[t] - ACT_BLOCKS[t]).then_inc(xbd_ready, 1)

            def new_w(t, count):
                r = slice(0, R[t])
                dve.wait_ge(x2_done, count)
                dve.wait_ge(xe_ready, count)
                stt(xw[r, t], ps[r, B_ITER(t), 0:C].rearrange("p (h c) -> p h c", c=ROWS), 2.0 / 49.0, xe[r, t],
                    ALU.mult, ALU.subtract).then_inc(w_ready, 1)

            def second_x2(t, count):
                r = slice(0, R[t])
                dve.wait_ge(x2h_ready, count)
                stt(x2_16[r, t, 1], ps[r, B_ITER(t), 0:C].rearrange("p (h c) -> p h c", c=ROWS), -1.0 / 7.0,
                    x2_16[r, t, 0], ALU.mult, ALU.subtract).then_inc(x2l_ready, 1)

            def spread_x2(t, count):
                dve.wait_ge(x2l_ready, count)
                spread(tt, bd2, x2_16, t, BLOCKS[t] - ACT_BLOCKS[t]).then_inc(x2bd_ready, 1)

            dve.wait_ge(gram_read, TILES)
            dve.wait_ge(at_done, 2 * TILES)
            for t in range(TILES):
                r = slice(0, R[t])
                ts(xm[r, t], xm[r, t], rscale[r, 0:1], ALPHA, ALU.mult, ALU.mult).then_inc(x_ready, 1)
                if t >= 1:
                    spread_x(t - 1, t)
            with dve.Fori(0, ITERS) as it:
                for t in range(TILES):
                    if t >= 1:
                        second_x2(t - 1, it * TILES + t)
                    new_w(t, it * TILES + (t + 1))
                    if t == 0:
                        spread_x(TILES - 1, it * TILES + TILES)
                    else:
                        spread_x2(t - 1, it * TILES + t)
                for t in range(TILES):
                    if t == 0:
                        second_x2(TILES - 1, it * TILES + TILES)
                    new_x(t, it * TILES + (t + 1))
                    if t == 0:
                        spread_x2(TILES - 1, it * TILES + TILES)
                    else:
                        spread_x(t - 1, it * TILES + (TILES + t))

            def rest_of_yv(t):
                r = slice(0, R[t])
                p = t % 2
                dve.wait_ge(yv1_ready, t + 1)
                if t >= 2:
                    dve.wait_ge(yv3_ready, t - 1)
                stt(yvrest[r, p], bank(B_YV(t), R[t], HEADS * D), 1.0 / ALPHA, yv3[r, p, 0], ALU.mult, ALU.subtract
                    ).then_inc(yvrest_ready, 1)

            def attention_out(t):
                r = slice(0, R[t])
                dve.wait_ge(att_done, t + 1)
                nc.vector.tensor_reduce(att[r], bank(B_ATT, R[t], 3 * D).rearrange("p (j d) -> p d j", j=3),
                                        AX, ALU.add).then_inc(h2_read, 1)
                dve.wait_ge(h2_read, t + 1)
                if t == 0:
                    dve.wait_ge(base_complete, 1)
                own(tt(h2[r, t, :], base[r, t, :], att[r], ALU.add))
                layernorm_stats(t, h2[r, t, :])
                ts(powarg[r, t, 0:1], moments[r, t, 1:2], EPS, None, ALU.add).then_inc(arg2_ready, 1)

            def normalise_h2(t):
                r = slice(0, R[t])
                dve.wait_ge(rstd2_ready, t + 1)
                ts(zn[r, t, :], h2[r, t, :], moments[r, t, 0:1], rstd[r, t, 0:1], ALU.subtract, ALU.mult
                   ).then_inc(zn_ready, 1)

            def choose(t):
                r = slice(0, R[t])
                shape = [R[t], EXPERTS, EXPERTS]
                dve.wait_ge(gate_done, t + 1)
                nc.vector.tensor_copy(gate[r, :], bank(B_MISC, R[t], EXPERTS)).then_inc(gate_read, 1)
                dve.wait_ge(gate_read, t + 1)
                other = gate[r, None, :].broadcast_to(shape)
                mine = gate[r, :, None].broadcast_to(shape)
                tied = ahead[r, 1]
                tt(ahead[r, 0], other, mine, ALU.is_gt).then_inc(choose_step, 1)
                own(tt(tied, other, mine, ALU.is_equal))
                own(tt(tied, tied, const("before", R[t]).rearrange("p (e j) -> p e j", e=EXPERTS), ALU.mult))
                dve.wait_ge(choose_step, t + 1)
                own(nc.vector.tensor_reduce(rank[r, :], ahead[r].rearrange("p k e j -> p e k j"),
                                            mybir.AxisListType.XY, ALU.add))
                ts(pick[r, t, :], rank[r, :], 2.0, None, ALU.is_lt).then_inc(pick_ready, 1)

            def pick_hidden(t, half):
                p = t % 2
                dve.wait_ge(pickb_done, 2 * t + half + 1)
                dve.wait_ge(hid_ready, 2 * t + half + 1)
                if t >= 2:
                    dve.wait_ge(ffn_done, t - 1)
                tt(hidm[:, p, 4 * half:4 * half + 4, 0:R[t]], hid[:, p, 4 * half:4 * half + 4, 0:R[t]],
                   bank(B_PICK + half, HIDDEN, 4 * R[t]).rearrange("p (e n) -> p e n", e=4), ALU.mult
                   ).then_inc(hidm_ready, 1)

            def result(t):
                r = slice(0, R[t])
                dve.wait_ge(ffn_done, t + 1)
                tt(res[r, t, :], h2[r, t, :], bank(B_FFN(t), R[t], D), ALU.add).then_inc(res_ready, 1)

            rest_of_yv(0)
            spread_x(TILES - 1, (ITERS + 1) * TILES)
            r = slice(0, R[0])
            dve.wait_ge(yv2_ready, 1)
            tt(yv3[r, 0, 2], yvrest[r, 0], yv3[r, 0, 1], ALU.subtract).then_inc(yv3_ready, 1)
            rest_of_yv(1)
            for s in range(1, TILES + 2):
                if s >= 2:
                    choose(s - 2)
                if s <= TILES:
                    attention_out(s - 1)
                    normalise_h2(s - 1)
                if s >= 2:
                    pick_hidden(s - 2, 0)
                    pick_hidden(s - 2, 1)
                if s + 1 < TILES:
                    rest_of_yv(s + 1)
                if s >= 2:
                    result(s - 2)

        @block.tensor
        def _(pe):
            mm = nc.tensor.matmul

            def parts_product(out, stationary, moving):
                steps = [(stationary[:, i], moving[:, j]) for i in range(stationary.shape[1])
                         for j in range(moving.shape[1])]
                for i, (lhsT, rhs) in enumerate(steps):
                    last = mm(out, lhsT, rhs, start=(i == 0), stop=(i == len(steps) - 1))
                return last

            def w_v_w_out():
                pe.wait_ge(wv_loaded, 16)
                for c in range(2):
                    last = mm(ps[0:D, B_WVO, c * 4 * D:(c + 1) * 4 * D], wvT[:, c, :], woutbd[:, c, :],
                              start=True, stop=True)
                last.then_inc(wvo_done, 1)

            def embed(t):
                pe.wait_ge(x_in_sem[t], 16)
                if t == 0:
                    pe.wait_ge(tokw_loaded, 16)
                if t >= 1:
                    pe.wait_ge(emb_read, t)
                if t >= 4:
                    pe.wait_ge(cols_ready, t - 3)
                for c in range(CHUNKS):
                    last = mm(bank(B_EMB, R[t], D), x_tile(t, c), tokw[:, c, :],
                              start=(c == 0), stop=(c == CHUNKS - 1))
                last.then_inc(emb_done, 1)

            def turn(t):
                pe.wait_ge(xc_ready, 2 * t + 1)
                if t == 0:
                    pe.wait_ge(cst_loaded, 16)
                if t >= 1:
                    pe.wait_ge(qk_ready, 5 * t)
                nc.tensor.transpose(bank(B_XT, D, R[t]), xc[0:R[t], t, :], ident[0:R[t], 0:R[t]]
                                    ).then_inc(xt_done, 1)

            def project(t):
                cols = xnT[:, OFF[t]:OFF[t] + R[t]]
                pe.wait_ge(xnT_ready, t + 1)
                if t == 0:
                    pe.wait_ge(p65_loaded, 16)
                    pe.wait_ge(pool_setup, filled("wvo"))
                if t >= 1:
                    pe.wait_ge(qk_ready, 5 * t)
                for c in range(2):
                    last = mm(ps[:, B_K, c * R[t]:(c + 1) * R[t]], wqk[:, 2 + c, :], cols, start=True, stop=True)
                last.then_inc(k_done, 1)
                if t >= 2:
                    pe.wait_ge(gram_read, t - 1)
                for c in range(2):
                    at = AT_Q + c * R[t]
                    last = mm(ps[:, B_Q, at:at + R[t]], wqk[:, c, :], cols, start=True, stop=True)
                last.then_inc(q_done, 1)
                if t == 0:
                    pe.wait_ge(wvo_ready, 1)
                if t >= 1:
                    pe.wait_ge(v_ready, t)
                mm(bank(B_V, R[t], HEADS * D), cols, wvo[:, :], start=True, stop=True).then_inc(v_done, 1)

            def scores(t):
                p = t % 2
                pe.wait_ge(qk_ready, 5 * (t + 1))
                if t == 0:
                    pe.wait_ge(setup_done, 2)
                for c in range(2):
                    if t >= 1:
                        pe.wait_ge(score_read, 2 * (t - 1) + c + 1)
                    out = bank(B_SCORE + c, R[t], 4 * R[t])
                    mm(out.rearrange("p (h n) -> p h n", h=4), farl[:, 0:R[t]], farr[:, :, 0:R[t]],
                       start=True, stop=False)
                    mm(out.rearrange("p (h n) -> p h n", h=4), qT[:, p, c, 0:R[t]], kT[:, p, c, :, 0:R[t]],
                       start=False, stop=True).then_inc(score_done, 1)

            def gram(t):
                r = slice(0, R[t])
                pe.wait_ge(a_ready, 2 * t + 1)
                if t >= 1:
                    pe.wait_ge(cols_ready, t)
                pe.wait_ge(emb_read, min(t + 4, TILES))
                mm(ps[0:BLOCKS[t], B_COLS, AT_COLS:AT_COLS + C], const("selw", R[t])[:, 0:BLOCKS[t]],
                   a[r, t].rearrange("p h c -> p (h c)"), start=True, stop=True).then_inc(cols_done, 1)
                if t == 0:
                    pe.wait_ge(pool_setup, filled("bd"))
                if t >= 1:
                    pe.wait_ge(gram_read, t)
                pe.wait_ge(xnT_ready, min(t + 3, TILES))
                pe.wait_ge(qk_ready, 5 * min(t + 2, TILES))
                pe.wait_ge(abd_ready, t + 1)
                pe.wait_ge(abd_act_ready, t + 1)
                for k in range(HEADS):
                    last = parts_product(ps[:, B_GRAM, k * ROWS:(k + 1) * ROWS], bd[r, t, :, k],
                                         a16[r, t, :, k])
                last.then_inc(gram_done, 1)

            def turn_a(t):
                r = slice(0, R[t])
                for part in range(2):
                    if t >= 1:
                        pe.wait_ge(at_ready, 2 * (t - 1) + part + 1)
                    out16 = ps[:, B_AT + part, :].bitcast(F16).rearrange("p (h n) -> p h n", h=HEADS)
                    for k in range(HEADS):
                        last = nc.tensor.transpose(out16[:, k, 0:R[t]], bd[r, t, part, k, :], ident16[r, r])
                    last.then_inc(at_done, 1)

            def convolution(heads):
                for k in heads:
                    last = mm(bank(B_TOEP, RMAX, TILES * D).rearrange("p (t d) -> p t d", t=TILES),
                              toepbd[:, k, :], v[:, :, k * D:(k + 1) * D], start=(k == 0), stop=(k == HEADS - 1))
                return last

            def keep_clock_up(n):
                for _ in range(n):
                    mm(bank(B_IDLE, 128, 512), xnT[:, 0:128], xnT[:, 0:512], start=True, stop=True)

            pe.wait_ge(pool_setup, filled("xnT"))
            keep_clock_up(2)
            embed(0)
            keep_clock_up(2)
            w_v_w_out()
            for s in range(TILES + 2):
                if s == 0:
                    turn(0)
                if s + 1 < TILES:
                    embed(s + 1)
                if 1 <= s < TILES:
                    turn(s)
                if 1 <= s <= TILES:
                    scores(s - 1)
                if s == TILES + 1:
                    pe.wait_ge(setup_done, 6)
                    pe.wait_ge(v_ready, TILES)
                    pe.wait_ge(qk_ready, 5 * TILES)
                    convolution(range(3))
                if s >= 2:
                    gram(s - 2)
                    turn_a(s - 2)
                if s < TILES:
                    project(s)
            pe.wait_ge(peak_ready, 1)
            nc.tensor.transpose(bank(B_PEAK, 2, RMAX), peak[:, :], ident[0:RMAX, 0:RMAX]
                                ).then_inc(peakT_done, 1)
            pe.wait_ge(peakd_ready, 1)
            mm(bank(B_PEAK, RMAX, 2), ones2[:, :], peakd[:, :], start=True, stop=True).then_inc(peakb_done, 1)
            convolution(range(3, HEADS)).then_inc(toep_done, 1)
            pe.wait_ge(at_ready, 2 * TILES)
            pe.wait_ge(pool_setup, filled("bd2"))

            with pe.Fori(0, ITERS) as it:
                for t in range(TILES):
                    r = slice(0, R[t])
                    pe.wait_ge(xbd_ready, it * TILES + (t + 1))
                    pe.wait_ge(xbd_act_ready, it * TILES + (t + 1))
                    for k in range(HEADS):
                        last = parts_product(ps[:, B_ITER(t), k * ROWS:(k + 1) * ROWS],
                                             bd[r, t, :, k], x16[r, t, :, k])
                    last.then_inc(x2_done, 1)
                for t in range(TILES):
                    r = slice(0, R[t])
                    pe.wait_ge(wl_ready, it * TILES + (t + 1))
                    pe.wait_ge(x2bd_ready, it * TILES + (t + 1))
                    pe.wait_ge(x2bd_act_ready, it * TILES + (t + 1))
                    for k in range(HEADS):
                        last = parts_product(ps[:, B_ITER(t), C + k * ROWS:C + (k + 1) * ROWS],
                                             bd2[r, t, :, k], w16[r, t, :, k])
                    last.then_inc(prod_done, 1)

            def x_times_v(t):
                r = slice(0, R[t])
                pe.wait_ge(xbd_ready, TILES * ITERS + t + 1)
                pe.wait_ge(xbd_act_ready, TILES * ITERS + t + 1)
                pe.wait_ge(v_cut, t + 1)
                if t >= 2:
                    pe.wait_ge(yvrest_ready, t - 1)
                if t == 1:
                    pe.wait_ge(conv_read, 1)
                if t >= 4:
                    pe.wait_ge(res_ready, t - 3)
                for k in range(HEADS):
                    last = parts_product(ps[:, B_YV(t), k * D:(k + 1) * D], bd[r, t, :, k],
                                         v3[r, t, :, k * D:(k + 1) * D])
                last.then_inc(yv_done, 1)

            def a_times(t):
                r = slice(0, R[t])
                pe.wait_ge(yv3_ready, t + 1)
                if t >= 1:
                    pe.wait_ge(h2_read, t)
                steps = [(k, i) for k in range(HEADS) for i in range(2)]
                for n, (k, i) in enumerate(steps):
                    last = mm(bank(B_ATT, 128, 3 * D).rearrange("p (j d) -> p j d", j=3), aT[r, t, i, k],
                              yv3[r, t % 2, :, k * D:(k + 1) * D], start=(n == 0), stop=(n == len(steps) - 1))
                last.then_inc(att_done, 1)

            def turn_z(t):
                pe.wait_ge(zn_ready, t + 1)
                if t >= 1:
                    pe.wait_ge(pickT_ready, 2 * t)
                nc.tensor.transpose(bank(B_MISC, D, R[t]), zn[0:R[t], t, :], ident[0:R[t], 0:R[t]]
                                    ).then_inc(zt_done, 1)

            def gates(t):
                if t == 0:
                    pe.wait_ge(bias_loaded, 32)
                    pe.wait_ge(ffn_loaded, 32)
                    pe.wait_ge(pool_setup, filled("zT"))
                pe.wait_ge(zT_ready, t + 1)
                mm(bank(B_MISC, R[t], EXPERTS), zT[:, t, 0:R[t]], wg, start=True, stop=True
                   ).then_inc(gate_done, 1)

            def up(t, half):
                if t >= 1:
                    pe.wait_ge(hid_ready, 2 * (t - 1) + half + 1)
                for k in range(4):
                    last = mm(ps[:, B_UP + half, k * R[t]:(k + 1) * R[t]], w1[:, 4 * half + k, :],
                              zT[:, t, 0:R[t]], start=True, stop=True)
                last.then_inc(up_done, 1)

            def turn_picks(t):
                pe.wait_ge(pick_ready, t + 1)
                nc.tensor.transpose(bank(B_MISC, EXPERTS, R[t]), pick[0:R[t], t, :], ident[0:R[t], 0:R[t]]
                                    ).then_inc(pickT_done, 1)

            def picks(t):
                pe.wait_ge(pickT_ready, 2 * t + 1)
                for half in range(2):
                    if t >= 1:
                        pe.wait_ge(hidm_ready, 2 * (t - 1) + half + 1)
                    for k in range(4):
                        last = mm(ps[:, B_PICK + half, k * R[t]:(k + 1) * R[t]], onehot[:, 4 * half + k, :],
                                  pickTb[:, t % 2, 0:R[t]], start=True, stop=True)
                    last.then_inc(pickb_done, 1)

            def down(t):
                out = bank(B_FFN(t), R[t], D)
                pe.wait_ge(yvrest_ready, min(t + 3, TILES))
                pe.wait_ge(pickT_ready, 2 * t + 2)
                mm(out, pickT[:, t % 2, 0:R[t]], b2[:, :], start=True, stop=False)
                for k in range(EXPERTS):
                    if k % 4 == 0:
                        pe.wait_ge(hidm_ready, 2 * t + k // 4 + 1)
                    last = mm(out, hidm[:, t % 2, k, 0:R[t]], w2[:, k, :], start=False, stop=(k == EXPERTS - 1))
                last.then_inc(ffn_done, 1)

            def yv_step(t):
                return max(1, t - 2) if t < 4 else t - 1

            x_times_v(0)
            x_times_v(1)
            for s in range(1, TILES + 2):
                if s >= 2:
                    gates(s - 2)
                if s == 1:
                    pe.wait_ge(x_ready, (ITERS + 1) * TILES)
                if s <= TILES:
                    a_times(s - 1)
                if s >= 2:
                    up(s - 2, 0)
                    turn_picks(s - 2)
                    up(s - 2, 1)
                    picks(s - 2)
                for t in range(2, TILES):
                    if yv_step(t) == s:
                        x_times_v(t)
                if s <= TILES:
                    turn_z(s - 1)
                if s >= 2:
                    down(s - 2)


def shape_constants():
    row = np.arange(RMAX)
    image, place = row // ROWS, row % ROWS
    w = np.where(place == 0, np.sqrt(PADS), 1.0)
    wc = np.where(np.arange(ROWS) == 0, np.sqrt(PADS), 1.0)
    parts = {}
    parts["ident"] = np.eye(128)
    parts["blocks"] = image[:, None] == image[None, :]
    parts["wcol"] = np.broadcast_to(wc * wc, (RMAX, ROWS))
    parts["wsym"] = w[:, None] / wc[None, :]
    parts["eye"] = 15.0 / 2.0 * (place[:, None] == np.arange(ROWS))
    parts["selw"] = w[:, None] * (image[:, None] == np.arange(PER_TILE))
    parts["before"] = np.broadcast_to(np.tril(np.ones((EXPERTS, EXPERTS)), -1).reshape(1, -1), (RMAX, EXPERTS ** 2))
    farl, farr = np.zeros((128, RMAX)), np.zeros((128, RMAX))
    for j in range(4):
        farl[32 * j] = -FAR / 4
        farr[32 * j] = 1.0
        for g in range(PER_TILE):
            farl[32 * j + 1 + g] = FAR / 4 * (image == g)
            farr[32 * j + 1 + g] = image == g
    parts["farl"], parts["farr"] = farl, farr
    cols, n = starts(CST)
    out = np.zeros((128, n), np.float32)
    for name, (lo, hi) in cols.items():
        out[:len(parts[name]), lo:hi] = parts[name]
    return out


def pack(rows, widths, parts):
    cols, n = starts(widths)
    out = np.zeros((rows, n), np.float32)
    for name, (lo, hi) in cols.items():
        out[:len(parts[name]), lo:hi] = parts[name]
    return out


def kernel(x, L0_tok_W, L0_tok_b, L0_attn_ln_g, L0_attn_ln_b, L0_attn_w_qkv, L0_attn_w_out, L0_attn_b_out,
           L0_attn_res_kernel, L0_ffn_Wg, L0_ffn_bg, L0_ffn_W1, L0_ffn_b1, L0_ffn_W2, L0_ffn_b2):
    import concourse.bacc as bacc
    from concourse.bass_utils import run_bass_kernel_spmd

    x, W, tok_b, g, b, w_qkv, w_out, b_out, rk, Wg, bg, W1, b1, W2, b2 = (np.asarray(i) for i in (
        x, L0_tok_W, L0_tok_b, L0_attn_ln_g, L0_attn_ln_b, L0_attn_w_qkv, L0_attn_w_out, L0_attn_b_out,
        L0_attn_res_kernel, L0_ffn_Wg, L0_ffn_bg, L0_ffn_W1, L0_ffn_b1, L0_ffn_W2, L0_ffn_b2))
    patches = x.reshape(IMAGES, 3, 4, 16, 4, 16).transpose(1, 3, 5, 0, 2, 4).reshape(CHUNKS, 128, IMAGES, TOKENS)
    rows = np.zeros((CHUNKS, 128, IMAGES, ROWS), np.float32)
    rows[..., 1:] = patches
    rows = rows.reshape(CHUNKS, 128, ALL_ROWS).transpose(1, 0, 2)
    x_l = np.concatenate([rows[:, :, OFF[t]:OFF[t] + R[t]].reshape(128, -1) for t in range(TILES)], axis=1)

    wout_bd = np.zeros((2, 4, DH, 4, D), np.float32)
    for j in range(4):
        wout_bd[:, j, :, j, :] = w_out.reshape(2, 4, DH, D)[:, j]
    toep = np.zeros((PER_TILE, ROWS, HEADS, ROWS), np.float32)
    for j in range(TOKENS):
        for i in range(TOKENS):
            toep[:, 1 + j, :, 1 + i] = rk[:, 0, j - i + 16, 0]
    p128 = pack(128, P128, dict(
        tokw=W.T.reshape(CHUNKS, 128, D).transpose(1, 0, 2).reshape(128, -1),
        wvT=w_qkv[:, 2 * HEADS * DH:].T.reshape(2, 128, D).transpose(1, 0, 2).reshape(128, -1),
        woutbd=wout_bd.reshape(2, 128, 4 * D).transpose(1, 0, 2).reshape(128, -1),
        w2=W2.transpose(1, 0, 2).reshape(HIDDEN, -1)))
    p65 = pack(D + 1, P65, dict(
        wqk=w_qkv[:, :2 * HEADS * DH],
        ln=np.stack([g, b], axis=1),
        wg=np.concatenate([Wg, bg[None, :]], axis=0),
        w1=np.concatenate([W1.transpose(1, 0, 2).reshape(D, -1), b1.reshape(1, -1)], axis=0)))
    p119 = pack(RMAX, P119, dict(
        tokb=np.broadcast_to(tok_b, (RMAX, D)), bout=np.broadcast_to(b_out, (RMAX, D)),
        toep=toep.reshape(RMAX, -1)))

    arrays = {"x_l": x_l, "p128": p128, "p65": p65, "p119": p119, "b2": np.ascontiguousarray(b2),
              "cst": shape_constants()}
    nc = bacc.Bacc("TRN2", target_bir_lowering=False, num_devices=1)
    args = [nc.dram_tensor(f"{n}_dram", a.shape, F32, kind="ExternalInput").ap() for n, a in arrays.items()]
    out = nc.dram_tensor("out_dram", [ALL_ROWS, D], F32, kind="ExternalOutput").ap()
    vit_layer(nc, *args, out)
    r = run_bass_kernel_spmd(nc, [{f"{n}_dram": a for n, a in arrays.items()}], core_ids=[0])
    got = r.results[0]["out_dram"]
    return np.ascontiguousarray(got.reshape(IMAGES, ROWS, D)[:, 1:, :])
```
